# Optimizing a Trainium2 kernel written in Bass

```python
import numpy as np
import jax
import jax.numpy as jnp

def _softmax(x, axis=-1):
    return jax.nn.softmax(x, axis=axis)

def _gelu(x):
    return jax.nn.gelu(x, approximate=True)

def _silu(x):
    return jax.nn.silu(x)

def _sigmoid(x):
    return jax.nn.sigmoid(x)

def _layernorm(x, axis=-1, eps=1e-05):
    m = jnp.mean(x, axis=axis, keepdims=True)
    v = jnp.var(x, axis=axis, keepdims=True)
    return (x - m) / jnp.sqrt(v + eps)

def _scatter_add(tgt, idx, src, axis=0):
    return tgt.at[idx].add(src)

def _segment_sum(src, seg, n):
    return jax.ops.segment_sum(src, seg, n)
kernel_name = 'mk_xattn_seq_d4_seqx_r4_5b475f'

def setup_inputs(seed: int=0):
    np.random.seed(seed)
    _w = jnp.asarray

    def _rec_inputs():
        import jax
        import jax.numpy as jnp
        _rk = jax.random.key(seed)
        x = -0.0002928 + 1 * jax.random.normal(jax.random.fold_in(_rk, 1), (8, 512, 256), jnp.float32)
        _lenS = 512 - jax.random.randint(jax.random.fold_in(_rk, 7), (8,), 0, max(1, 512 // 4) + 1, jnp.int32)
        _lenS2 = 512 - jax.random.randint(jax.random.fold_in(_rk, 8), (8,), 0, max(1, 512 // 4) + 1, jnp.int32)
        _ctx_1024P = jax.random.normal(jax.random.fold_in(_rk, 11), (8, 16, 256), jnp.float32)
        _ctx_1024c = jax.random.dirichlet(jax.random.fold_in(_rk, 511), 0.3 * jnp.ones((16,), jnp.float32), (8, 512))
        _ctx_1024t = jnp.einsum('bsk,bkd->bsd', _ctx_1024c, _ctx_1024P)
        _ctx_1024t = _ctx_1024t * jax.lax.rsqrt(jnp.mean(jnp.square(_ctx_1024t)) + 1e-12) * 0.953939
        ctx_1024 = -1.39393e-06 + 0.999914 * (_ctx_1024t + 0.3 * jax.random.normal(jax.random.fold_in(_rk, 611), (8, 512, 256), jnp.float32))
        return (x, ctx_1024)
    x, ctx_1024 = _rec_inputs()

    def _L0_xattn_setup():
        import jax, jax.numpy as jnp
        import numpy as np
        B, L, M, D, H, FF, W = (2, 512, 512, 256, 16, 1024, 64)
        DH = D // H

        def _layernorm(x, g, b, eps=1e-05):
            mu = x.mean(-1, keepdims=True)
            var = ((x - mu) ** 2).mean(-1, keepdims=True)
            return (x - mu) / jnp.sqrt(var + eps) * g + b

        def _mha(qx, kx, wq, bq, wk, bk, wv, bv, wo, bo, mask, bias):
            Bq, Lq, _ = qx.shape
            Lk = kx.shape[1]
            q = (qx @ wq + bq).reshape(Bq, Lq, H, DH).transpose(0, 2, 1, 3)
            k = (kx @ wk + bk).reshape(Bq, Lk, H, DH).transpose(0, 2, 1, 3)
            v = (kx @ wv + bv).reshape(Bq, Lk, H, DH).transpose(0, 2, 1, 3)
            s = jnp.einsum('bhqd,bhkd->bhqk', q, k) / jnp.sqrt(jnp.asarray(DH, qx.dtype))
            if bias is not None:
                s = s + bias[None]
            if mask is not None:
                s = jnp.where(mask[None, None], s, jnp.asarray(-1000000000.0, qx.dtype))
            a = jax.nn.softmax(s, axis=-1)
            o = jnp.einsum('bhqk,bhkd->bhqd', a, v).transpose(0, 2, 1, 3).reshape(Bq, Lq, D)
            return o @ wo + bo

        def _forward(x, mem, swq, sbq, swk, sbk, swv, sbv, swo, sbo, cwq, cbq, cwk, cbk, cwv, cbv, cwo, cbo, w1, b1, w2, b2, g1, be1, g2, be2, g3, be3):
            i = jnp.arange(L)[:, None]
            j = jnp.arange(L)[None, :]
            mask = (j <= i) & (i - j < W)
            slopes = 2.0 ** (-8.0 * jnp.arange(1, H + 1, dtype=x.dtype) / H)
            bias = slopes[:, None, None] * (j - i).astype(x.dtype)[None]
            sa = _mha(x, x, swq, sbq, swk, sbk, swv, sbv, swo, sbo, mask, bias)
            x = _layernorm(x + sa, g1, be1)
            ca = _mha(x, mem, cwq, cbq, cwk, cbk, cwv, cbv, cwo, cbo, None, None)
            x = _layernorm(x + ca, g2, be2)
            ff = jax.nn.gelu(x @ w1 + b1, approximate=False) @ w2 + b2
            return _layernorm(x + ff, g3, be3)
        key = jax.random.key(seed)
        ks = jax.random.split(key, 16)
        s = 0.02
        inp = {'x': jax.random.normal(ks[0], (B, L, D), jnp.float32), 'mem': jax.random.normal(ks[1], (B, M, D), jnp.float32)}
        for n, k in zip(['swq', 'swk', 'swv', 'swo'], jax.random.split(ks[2], 4)):
            inp[n] = jax.random.normal(k, (D, D), jnp.float32) * s
        for n in ['sbq', 'sbk', 'sbv', 'sbo']:
            inp[n] = jnp.zeros((D,), jnp.float32)
        for n, k in zip(['cwq', 'cwk', 'cwv', 'cwo'], jax.random.split(ks[3], 4)):
            inp[n] = jax.random.normal(k, (D, D), jnp.float32) * s
        for n in ['cbq', 'cbk', 'cbv', 'cbo']:
            inp[n] = jnp.zeros((D,), jnp.float32)
        inp['w1'] = jax.random.normal(ks[4], (D, FF), jnp.float32) * s
        inp['b1'] = jnp.zeros((FF,), jnp.float32)
        inp['w2'] = jax.random.normal(ks[5], (FF, D), jnp.float32) * s
        inp['b2'] = jnp.zeros((D,), jnp.float32)
        for n in ['g1', 'g2', 'g3']:
            inp[n] = jnp.ones((D,), jnp.float32)
        for n in ['be1', 'be2', 'be3']:
            inp[n] = jnp.zeros((D,), jnp.float32)
        return inp
    _L0_xattn_all = _L0_xattn_setup()
    _L0_xattn_in = {k: v for k, v in _L0_xattn_all.items() if k in ('swq', 'sbq', 'swk', 'sbk', 'swv', 'sbv', 'swo', 'sbo', 'cwq', 'cbq', 'cwk', 'cbk', 'cwv', 'cbv', 'cwo', 'cbo', 'w1', 'b1', 'w2', 'b2', 'g1', 'be1', 'g2', 'be2', 'g3', 'be3')}
    del _L0_xattn_all

    def _L1_xattn_setup():
        import math
        import jax, jax.numpy as jnp
        import numpy as np
        D_MODEL = 256
        EMB = 256
        H = 16
        HD = D_MODEL // H
        B = 2
        S = 512

        def _ln(x, g, b, eps=1e-05):
            m = jnp.mean(x, axis=-1, keepdims=True)
            v = jnp.var(x, axis=-1, keepdims=True)
            return (x - m) * jax.lax.rsqrt(v + eps) * g + b

        def _mha(xq, xk, xv, Wq, bq, Wk, bk, Wv, bv, Wo, bo, causal):
            q = jnp.einsum('bsd,hed->bhse', xq, Wq) + bq[None, :, None, :]
            k = jnp.einsum('bsd,hed->bhse', xk, Wk) + bk[None, :, None, :]
            v = jnp.einsum('bsd,hed->bhse', xv, Wv) + bv[None, :, None, :]
            s = jnp.einsum('bhqe,bhke->bhqk', q, k) * (1.0 / math.sqrt(D_MODEL))
            if causal:
                Lq, Lk = (s.shape[-2], s.shape[-1])
                mask = jnp.tril(jnp.ones((Lq, Lk), dtype=bool))
                s = jnp.where(mask, s, -jnp.inf)
            w = jax.nn.softmax(s, axis=-1)
            o = jnp.einsum('bhqk,bhke->bhqe', w, v)
            b_, h_, s_, e_ = o.shape
            o = o.transpose(0, 2, 1, 3).reshape(b_, s_, h_ * e_)
            return o @ Wo.T + bo

        def _forward(x, encoder_output, sa_q_W, sa_q_b, sa_k_W, sa_k_b, sa_v_W, sa_v_b, ca_q_W, ca_q_b, ca_k_W, ca_k_b, ca_v_W, ca_v_b, m_Wq, m_bq, m_Wk, m_bk, m_Wv, m_bv, m_Wo, m_bo, c_Wq, c_bq, c_Wk, c_bk, c_Wv, c_bv, c_Wo, c_bo, ff_W1, ff_b1, ff_W2, ff_b2, ln1_g, ln1_b, ln2_g, ln2_b, ln3_g, ln3_b):
            q = x @ sa_q_W.T + sa_q_b
            k = x @ sa_k_W.T + sa_k_b
            v = x @ sa_v_W.T + sa_v_b
            sa = _mha(q, k, v, m_Wq, m_bq, m_Wk, m_bk, m_Wv, m_bv, m_Wo, m_bo, causal=True)
            x = _ln(x + sa, ln1_g, ln1_b)
            q = x @ ca_q_W.T + ca_q_b
            k = encoder_output @ ca_k_W.T + ca_k_b
            v = encoder_output @ ca_v_W.T + ca_v_b
            ca = _mha(q, k, v, c_Wq, c_bq, c_Wk, c_bk, c_Wv, c_bv, c_Wo, c_bo, causal=False)
            x = _ln(x + ca, ln2_g, ln2_b)
            h = jax.nn.gelu(x @ ff_W1.T + ff_b1, approximate=False)
            ff = h @ ff_W2.T + ff_b2
            x = _ln(x + ff, ln3_g, ln3_b)
            return x
        key = jax.random.key(seed)
        ks = iter(jax.random.split(key, 64))
        p = lambda *shape: jax.random.normal(next(ks), shape, dtype=jnp.float32) * 0.02
        inp = {'x': jax.random.normal(next(ks), (B, S, EMB), dtype=jnp.float32), 'encoder_output': jax.random.normal(next(ks), (B, S, D_MODEL), dtype=jnp.float32), 'sa_q_W': p(D_MODEL, EMB), 'sa_q_b': p(D_MODEL), 'sa_k_W': p(D_MODEL, EMB), 'sa_k_b': p(D_MODEL), 'sa_v_W': p(D_MODEL, EMB), 'sa_v_b': p(D_MODEL), 'ca_q_W': p(D_MODEL, D_MODEL), 'ca_q_b': p(D_MODEL), 'ca_k_W': p(D_MODEL, D_MODEL), 'ca_k_b': p(D_MODEL), 'ca_v_W': p(D_MODEL, D_MODEL), 'ca_v_b': p(D_MODEL), 'm_Wq': p(H, HD, D_MODEL), 'm_bq': p(H, HD), 'm_Wk': p(H, HD, D_MODEL), 'm_bk': p(H, HD), 'm_Wv': p(H, HD, D_MODEL), 'm_bv': p(H, HD), 'm_Wo': p(D_MODEL, D_MODEL), 'm_bo': p(D_MODEL), 'c_Wq': p(H, HD, D_MODEL), 'c_bq': p(H, HD), 'c_Wk': p(H, HD, D_MODEL), 'c_bk': p(H, HD), 'c_Wv': p(H, HD, D_MODEL), 'c_bv': p(H, HD), 'c_Wo': p(D_MODEL, D_MODEL), 'c_bo': p(D_MODEL), 'ff_W1': p(4 * D_MODEL, D_MODEL), 'ff_b1': p(4 * D_MODEL), 'ff_W2': p(D_MODEL, 4 * D_MODEL), 'ff_b2': p(D_MODEL), 'ln1_g': jnp.ones((D_MODEL,), jnp.float32), 'ln1_b': jnp.zeros((D_MODEL,), jnp.float32), 'ln2_g': jnp.ones((D_MODEL,), jnp.float32), 'ln2_b': jnp.zeros((D_MODEL,), jnp.float32), 'ln3_g': jnp.ones((D_MODEL,), jnp.float32), 'ln3_b': jnp.zeros((D_MODEL,), jnp.float32)}
        return inp
    _L1_xattn_all = _L1_xattn_setup()
    _L1_xattn_in = {k: v for k, v in _L1_xattn_all.items() if k in ('sa_q_W', 'sa_q_b', 'sa_k_W', 'sa_k_b', 'sa_v_W', 'sa_v_b', 'ca_q_W', 'ca_q_b', 'ca_k_W', 'ca_k_b', 'ca_v_W', 'ca_v_b', 'm_Wq', 'm_bq', 'm_Wk', 'm_bk', 'm_Wv', 'm_bv', 'm_Wo', 'm_bo', 'c_Wq', 'c_bq', 'c_Wk', 'c_bk', 'c_Wv', 'c_bv', 'c_Wo', 'c_bo', 'ff_W1', 'ff_b1', 'ff_W2', 'ff_b2', 'ln1_g', 'ln1_b', 'ln2_g', 'ln2_b', 'ln3_g', 'ln3_b')}
    del _L1_xattn_all

    def _L2_xattn_setup():
        import jax, jax.numpy as jnp
        import numpy as np
        D = 256
        H = 16
        HD = D // H
        DFF = 4 * D
        LN_EPS = 1e-05

        def layernorm(x, gamma, beta):
            mu = jnp.mean(x, axis=-1, keepdims=True)
            var = jnp.mean(jnp.square(x - mu), axis=-1, keepdims=True)
            return (x - mu) * jax.lax.rsqrt(var + LN_EPS) * gamma + beta
        key = jax.random.key(seed)
        ks = jax.random.split(key, 10)
        B, Nq, Nk = (2, 512, 512)
        s = 0.02
        return {'q_x': jax.random.normal(ks[0], (B, Nq, D), jnp.float32), 'kv_x': jax.random.normal(ks[1], (B, Nk, D), jnp.float32), 'Wq': jax.random.normal(ks[2], (D, D), jnp.float32) * s, 'Wkv': jax.random.normal(ks[3], (2 * D, D), jnp.float32) * s, 'Wo': jax.random.normal(ks[4], (D, D), jnp.float32) * s, 'bo': jnp.zeros((D,), jnp.float32), 'ln_q_g': jnp.ones((D,), jnp.float32), 'ln_q_b': jnp.zeros((D,), jnp.float32), 'ln_kv_g': jnp.ones((D,), jnp.float32), 'ln_kv_b': jnp.zeros((D,), jnp.float32), 'W1': jax.random.normal(ks[5], (DFF, D), jnp.float32) * s, 'b1': jnp.zeros((DFF,), jnp.float32), 'W2': jax.random.normal(ks[6], (D, DFF), jnp.float32) * s, 'b2': jnp.zeros((D,), jnp.float32)}
    _L2_xattn_all = _L2_xattn_setup()
    _L2_xattn_in = {k: v for k, v in _L2_xattn_all.items() if k in ('Wq', 'Wkv', 'Wo', 'bo', 'ln_q_g', 'ln_q_b', 'ln_kv_g', 'ln_kv_b', 'W1', 'b1', 'W2', 'b2')}
    del _L2_xattn_all

    def _L3_xattn_setup():
        import jax, jax.numpy as jnp
        import numpy as np
        D_MODEL = 256
        NUM_HEADS = 16
        D_K = D_MODEL // NUM_HEADS
        BATCH = 4
        SEQ = 512

        def _layer_norm(x, gamma, beta, eps=1e-05):
            mu = jnp.mean(x, axis=-1, keepdims=True)
            var = jnp.var(x, axis=-1, keepdims=True)
            return (x - mu) * jax.lax.rsqrt(var + eps) * gamma + beta
        key = jax.random.key(seed)
        ks = jax.random.split(key, 16)
        s = 0.02
        return {'query': jax.random.normal(ks[0], (BATCH, SEQ, D_MODEL), jnp.float32), 'key': jax.random.normal(ks[1], (BATCH, SEQ, D_MODEL), jnp.float32), 'value': jax.random.normal(ks[2], (BATCH, SEQ, D_MODEL), jnp.float32), 'Wq': jax.random.normal(ks[3], (D_MODEL, D_MODEL), jnp.float32) * s, 'bq': jnp.zeros((D_MODEL,), jnp.float32), 'Wk': jax.random.normal(ks[4], (D_MODEL, D_MODEL), jnp.float32) * s, 'bk': jnp.zeros((D_MODEL,), jnp.float32), 'Wv': jax.random.normal(ks[5], (D_MODEL, D_MODEL), jnp.float32) * s, 'bv': jnp.zeros((D_MODEL,), jnp.float32), 'Wo': jax.random.normal(ks[6], (D_MODEL, D_MODEL), jnp.float32) * s, 'bo': jnp.zeros((D_MODEL,), jnp.float32), 'gamma': jnp.ones((D_MODEL,), jnp.float32), 'beta': jnp.zeros((D_MODEL,), jnp.float32)}
    _L3_xattn_all = _L3_xattn_setup()
    _L3_xattn_in = {k: v for k, v in _L3_xattn_all.items() if k in ('Wq', 'bq', 'Wk', 'bk', 'Wv', 'bv', 'Wo', 'bo', 'gamma', 'beta')}
    del _L3_xattn_all
    return {'x': x, 'ctx_1024': ctx_1024, 'L0_xattn_swq': _L0_xattn_in['swq'], 'L0_xattn_sbq': _L0_xattn_in['sbq'], 'L0_xattn_swk': _L0_xattn_in['swk'], 'L0_xattn_sbk': _L0_xattn_in['sbk'], 'L0_xattn_swv': _L0_xattn_in['swv'], 'L0_xattn_sbv': _L0_xattn_in['sbv'], 'L0_xattn_swo': _L0_xattn_in['swo'], 'L0_xattn_sbo': _L0_xattn_in['sbo'], 'L0_xattn_cwq': _L0_xattn_in['cwq'], 'L0_xattn_cbq': _L0_xattn_in['cbq'], 'L0_xattn_cwk': _L0_xattn_in['cwk'], 'L0_xattn_cbk': _L0_xattn_in['cbk'], 'L0_xattn_cwv': _L0_xattn_in['cwv'], 'L0_xattn_cbv': _L0_xattn_in['cbv'], 'L0_xattn_cwo': _L0_xattn_in['cwo'], 'L0_xattn_cbo': _L0_xattn_in['cbo'], 'L0_xattn_w1': _L0_xattn_in['w1'], 'L0_xattn_b1': _L0_xattn_in['b1'], 'L0_xattn_w2': _L0_xattn_in['w2'], 'L0_xattn_b2': _L0_xattn_in['b2'], 'L0_xattn_g1': _L0_xattn_in['g1'], 'L0_xattn_be1': _L0_xattn_in['be1'], 'L0_xattn_g2': _L0_xattn_in['g2'], 'L0_xattn_be2': _L0_xattn_in['be2'], 'L0_xattn_g3': _L0_xattn_in['g3'], 'L0_xattn_be3': _L0_xattn_in['be3'], 'L1_xattn_sa_q_W': _L1_xattn_in['sa_q_W'], 'L1_xattn_sa_q_b': _L1_xattn_in['sa_q_b'], 'L1_xattn_sa_k_W': _L1_xattn_in['sa_k_W'], 'L1_xattn_sa_k_b': _L1_xattn_in['sa_k_b'], 'L1_xattn_sa_v_W': _L1_xattn_in['sa_v_W'], 'L1_xattn_sa_v_b': _L1_xattn_in['sa_v_b'], 'L1_xattn_ca_q_W': _L1_xattn_in['ca_q_W'], 'L1_xattn_ca_q_b': _L1_xattn_in['ca_q_b'], 'L1_xattn_ca_k_W': _L1_xattn_in['ca_k_W'], 'L1_xattn_ca_k_b': _L1_xattn_in['ca_k_b'], 'L1_xattn_ca_v_W': _L1_xattn_in['ca_v_W'], 'L1_xattn_ca_v_b': _L1_xattn_in['ca_v_b'], 'L1_xattn_m_Wq': _L1_xattn_in['m_Wq'], 'L1_xattn_m_bq': _L1_xattn_in['m_bq'], 'L1_xattn_m_Wk': _L1_xattn_in['m_Wk'], 'L1_xattn_m_bk': _L1_xattn_in['m_bk'], 'L1_xattn_m_Wv': _L1_xattn_in['m_Wv'], 'L1_xattn_m_bv': _L1_xattn_in['m_bv'], 'L1_xattn_m_Wo': _L1_xattn_in['m_Wo'], 'L1_xattn_m_bo': _L1_xattn_in['m_bo'], 'L1_xattn_c_Wq': _L1_xattn_in['c_Wq'], 'L1_xattn_c_bq': _L1_xattn_in['c_bq'], 'L1_xattn_c_Wk': _L1_xattn_in['c_Wk'], 'L1_xattn_c_bk': _L1_xattn_in['c_bk'], 'L1_xattn_c_Wv': _L1_xattn_in['c_Wv'], 'L1_xattn_c_bv': _L1_xattn_in['c_bv'], 'L1_xattn_c_Wo': _L1_xattn_in['c_Wo'], 'L1_xattn_c_bo': _L1_xattn_in['c_bo'], 'L1_xattn_ff_W1': _L1_xattn_in['ff_W1'], 'L1_xattn_ff_b1': _L1_xattn_in['ff_b1'], 'L1_xattn_ff_W2': _L1_xattn_in['ff_W2'], 'L1_xattn_ff_b2': _L1_xattn_in['ff_b2'], 'L1_xattn_ln1_g': _L1_xattn_in['ln1_g'], 'L1_xattn_ln1_b': _L1_xattn_in['ln1_b'], 'L1_xattn_ln2_g': _L1_xattn_in['ln2_g'], 'L1_xattn_ln2_b': _L1_xattn_in['ln2_b'], 'L1_xattn_ln3_g': _L1_xattn_in['ln3_g'], 'L1_xattn_ln3_b': _L1_xattn_in['ln3_b'], 'L2_xattn_Wq': _L2_xattn_in['Wq'], 'L2_xattn_Wkv': _L2_xattn_in['Wkv'], 'L2_xattn_Wo': _L2_xattn_in['Wo'], 'L2_xattn_bo': _L2_xattn_in['bo'], 'L2_xattn_ln_q_g': _L2_xattn_in['ln_q_g'], 'L2_xattn_ln_q_b': _L2_xattn_in['ln_q_b'], 'L2_xattn_ln_kv_g': _L2_xattn_in['ln_kv_g'], 'L2_xattn_ln_kv_b': _L2_xattn_in['ln_kv_b'], 'L2_xattn_W1': _L2_xattn_in['W1'], 'L2_xattn_b1': _L2_xattn_in['b1'], 'L2_xattn_W2': _L2_xattn_in['W2'], 'L2_xattn_b2': _L2_xattn_in['b2'], 'L3_xattn_Wq': _L3_xattn_in['Wq'], 'L3_xattn_bq': _L3_xattn_in['bq'], 'L3_xattn_Wk': _L3_xattn_in['Wk'], 'L3_xattn_bk': _L3_xattn_in['bk'], 'L3_xattn_Wv': _L3_xattn_in['Wv'], 'L3_xattn_bv': _L3_xattn_in['bv'], 'L3_xattn_Wo': _L3_xattn_in['Wo'], 'L3_xattn_bo': _L3_xattn_in['bo'], 'L3_xattn_gamma': _L3_xattn_in['gamma'], 'L3_xattn_beta': _L3_xattn_in['beta']}

def reference(x, ctx_1024, L0_xattn_swq, L0_xattn_sbq, L0_xattn_swk, L0_xattn_sbk, L0_xattn_swv, L0_xattn_sbv, L0_xattn_swo, L0_xattn_sbo, L0_xattn_cwq, L0_xattn_cbq, L0_xattn_cwk, L0_xattn_cbk, L0_xattn_cwv, L0_xattn_cbv, L0_xattn_cwo, L0_xattn_cbo, L0_xattn_w1, L0_xattn_b1, L0_xattn_w2, L0_xattn_b2, L0_xattn_g1, L0_xattn_be1, L0_xattn_g2, L0_xattn_be2, L0_xattn_g3, L0_xattn_be3, L1_xattn_sa_q_W, L1_xattn_sa_q_b, L1_xattn_sa_k_W, L1_xattn_sa_k_b, L1_xattn_sa_v_W, L1_xattn_sa_v_b, L1_xattn_ca_q_W, L1_xattn_ca_q_b, L1_xattn_ca_k_W, L1_xattn_ca_k_b, L1_xattn_ca_v_W, L1_xattn_ca_v_b, L1_xattn_m_Wq, L1_xattn_m_bq, L1_xattn_m_Wk, L1_xattn_m_bk, L1_xattn_m_Wv, L1_xattn_m_bv, L1_xattn_m_Wo, L1_xattn_m_bo, L1_xattn_c_Wq, L1_xattn_c_bq, L1_xattn_c_Wk, L1_xattn_c_bk, L1_xattn_c_Wv, L1_xattn_c_bv, L1_xattn_c_Wo, L1_xattn_c_bo, L1_xattn_ff_W1, L1_xattn_ff_b1, L1_xattn_ff_W2, L1_xattn_ff_b2, L1_xattn_ln1_g, L1_xattn_ln1_b, L1_xattn_ln2_g, L1_xattn_ln2_b, L1_xattn_ln3_g, L1_xattn_ln3_b, L2_xattn_Wq, L2_xattn_Wkv, L2_xattn_Wo, L2_xattn_bo, L2_xattn_ln_q_g, L2_xattn_ln_q_b, L2_xattn_ln_kv_g, L2_xattn_ln_kv_b, L2_xattn_W1, L2_xattn_b1, L2_xattn_W2, L2_xattn_b2, L3_xattn_Wq, L3_xattn_bq, L3_xattn_Wk, L3_xattn_bk, L3_xattn_Wv, L3_xattn_bv, L3_xattn_Wo, L3_xattn_bo, L3_xattn_gamma, L3_xattn_beta):
    import jax
    import jax.numpy as jnp

    def _L0_xattn_ref(x, mem, swq, sbq, swk, sbk, swv, sbv, swo, sbo, cwq, cbq, cwk, cbk, cwv, cbv, cwo, cbo, w1, b1, w2, b2, g1, be1, g2, be2, g3, be3):
        import jax, jax.numpy as jnp
        import numpy as np
        B, L, M, D, H, FF, W = (2, 512, 512, 256, 16, 1024, 64)
        DH = D // H

        def _layernorm(x, g, b, eps=1e-05):
            mu = x.mean(-1, keepdims=True)
            var = ((x - mu) ** 2).mean(-1, keepdims=True)
            return (x - mu) / jnp.sqrt(var + eps) * g + b

        def _mha(qx, kx, wq, bq, wk, bk, wv, bv, wo, bo, mask, bias):
            Bq, Lq, _ = qx.shape
            Lk = kx.shape[1]
            q = (qx @ wq + bq).reshape(Bq, Lq, H, DH).transpose(0, 2, 1, 3)
            k = (kx @ wk + bk).reshape(Bq, Lk, H, DH).transpose(0, 2, 1, 3)
            v = (kx @ wv + bv).reshape(Bq, Lk, H, DH).transpose(0, 2, 1, 3)
            s = jnp.einsum('bhqd,bhkd->bhqk', q, k) / jnp.sqrt(jnp.asarray(DH, qx.dtype))
            if bias is not None:
                s = s + bias[None]
            if mask is not None:
                s = jnp.where(mask[None, None], s, jnp.asarray(-1000000000.0, qx.dtype))
            a = jax.nn.softmax(s, axis=-1)
            o = jnp.einsum('bhqk,bhkd->bhqd', a, v).transpose(0, 2, 1, 3).reshape(Bq, Lq, D)
            return o @ wo + bo

        def _forward(x, mem, swq, sbq, swk, sbk, swv, sbv, swo, sbo, cwq, cbq, cwk, cbk, cwv, cbv, cwo, cbo, w1, b1, w2, b2, g1, be1, g2, be2, g3, be3):
            i = jnp.arange(L)[:, None]
            j = jnp.arange(L)[None, :]
            mask = (j <= i) & (i - j < W)
            slopes = 2.0 ** (-8.0 * jnp.arange(1, H + 1, dtype=x.dtype) / H)
            bias = slopes[:, None, None] * (j - i).astype(x.dtype)[None]
            sa = _mha(x, x, swq, sbq, swk, sbk, swv, sbv, swo, sbo, mask, bias)
            x = _layernorm(x + sa, g1, be1)
            ca = _mha(x, mem, cwq, cbq, cwk, cbk, cwv, cbv, cwo, cbo, None, None)
            x = _layernorm(x + ca, g2, be2)
            ff = jax.nn.gelu(x @ w1 + b1, approximate=False) @ w2 + b2
            return _layernorm(x + ff, g3, be3)
        return _forward(x, mem, swq, sbq, swk, sbk, swv, sbv, swo, sbo, cwq, cbq, cwk, cbk, cwv, cbv, cwo, cbo, w1, b1, w2, b2, g1, be1, g2, be2, g3, be3)

    def _L1_xattn_ref(x, encoder_output, sa_q_W, sa_q_b, sa_k_W, sa_k_b, sa_v_W, sa_v_b, ca_q_W, ca_q_b, ca_k_W, ca_k_b, ca_v_W, ca_v_b, m_Wq, m_bq, m_Wk, m_bk, m_Wv, m_bv, m_Wo, m_bo, c_Wq, c_bq, c_Wk, c_bk, c_Wv, c_bv, c_Wo, c_bo, ff_W1, ff_b1, ff_W2, ff_b2, ln1_g, ln1_b, ln2_g, ln2_b, ln3_g, ln3_b):
        import math
        import jax, jax.numpy as jnp
        import numpy as np
        D_MODEL = 256
        EMB = 256
        H = 16
        HD = D_MODEL // H
        B = 2
        S = 512

        def _ln(x, g, b, eps=1e-05):
            m = jnp.mean(x, axis=-1, keepdims=True)
            v = jnp.var(x, axis=-1, keepdims=True)
            return (x - m) * jax.lax.rsqrt(v + eps) * g + b

        def _mha(xq, xk, xv, Wq, bq, Wk, bk, Wv, bv, Wo, bo, causal):
            q = jnp.einsum('bsd,hed->bhse', xq, Wq) + bq[None, :, None, :]
            k = jnp.einsum('bsd,hed->bhse', xk, Wk) + bk[None, :, None, :]
            v = jnp.einsum('bsd,hed->bhse', xv, Wv) + bv[None, :, None, :]
            s = jnp.einsum('bhqe,bhke->bhqk', q, k) * (1.0 / math.sqrt(D_MODEL))
            if causal:
                Lq, Lk = (s.shape[-2], s.shape[-1])
                mask = jnp.tril(jnp.ones((Lq, Lk), dtype=bool))
                s = jnp.where(mask, s, -jnp.inf)
            w = jax.nn.softmax(s, axis=-1)
            o = jnp.einsum('bhqk,bhke->bhqe', w, v)
            b_, h_, s_, e_ = o.shape
            o = o.transpose(0, 2, 1, 3).reshape(b_, s_, h_ * e_)
            return o @ Wo.T + bo

        def _forward(x, encoder_output, sa_q_W, sa_q_b, sa_k_W, sa_k_b, sa_v_W, sa_v_b, ca_q_W, ca_q_b, ca_k_W, ca_k_b, ca_v_W, ca_v_b, m_Wq, m_bq, m_Wk, m_bk, m_Wv, m_bv, m_Wo, m_bo, c_Wq, c_bq, c_Wk, c_bk, c_Wv, c_bv, c_Wo, c_bo, ff_W1, ff_b1, ff_W2, ff_b2, ln1_g, ln1_b, ln2_g, ln2_b, ln3_g, ln3_b):
            q = x @ sa_q_W.T + sa_q_b
            k = x @ sa_k_W.T + sa_k_b
            v = x @ sa_v_W.T + sa_v_b
            sa = _mha(q, k, v, m_Wq, m_bq, m_Wk, m_bk, m_Wv, m_bv, m_Wo, m_bo, causal=True)
            x = _ln(x + sa, ln1_g, ln1_b)
            q = x @ ca_q_W.T + ca_q_b
            k = encoder_output @ ca_k_W.T + ca_k_b
            v = encoder_output @ ca_v_W.T + ca_v_b
            ca = _mha(q, k, v, c_Wq, c_bq, c_Wk, c_bk, c_Wv, c_bv, c_Wo, c_bo, causal=False)
            x = _ln(x + ca, ln2_g, ln2_b)
            h = jax.nn.gelu(x @ ff_W1.T + ff_b1, approximate=False)
            ff = h @ ff_W2.T + ff_b2
            x = _ln(x + ff, ln3_g, ln3_b)
            return x
        return _forward(x, encoder_output, sa_q_W, sa_q_b, sa_k_W, sa_k_b, sa_v_W, sa_v_b, ca_q_W, ca_q_b, ca_k_W, ca_k_b, ca_v_W, ca_v_b, m_Wq, m_bq, m_Wk, m_bk, m_Wv, m_bv, m_Wo, m_bo, c_Wq, c_bq, c_Wk, c_bk, c_Wv, c_bv, c_Wo, c_bo, ff_W1, ff_b1, ff_W2, ff_b2, ln1_g, ln1_b, ln2_g, ln2_b, ln3_g, ln3_b)

    def _L2_xattn_ref(q_x, kv_x, Wq, Wkv, Wo, bo, ln_q_g, ln_q_b, ln_kv_g, ln_kv_b, W1, b1, W2, b2):
        import jax, jax.numpy as jnp
        import numpy as np
        D = 256
        H = 16
        HD = D // H
        DFF = 4 * D
        LN_EPS = 1e-05

        def layernorm(x, gamma, beta):
            mu = jnp.mean(x, axis=-1, keepdims=True)
            var = jnp.mean(jnp.square(x - mu), axis=-1, keepdims=True)
            return (x - mu) * jax.lax.rsqrt(var + LN_EPS) * gamma + beta
        B, Nq, _ = q_x.shape
        Nk = kv_x.shape[1]
        scale = HD ** (-0.5)
        q = layernorm(q_x, ln_q_g, ln_q_b) @ Wq.T
        kv = layernorm(kv_x, ln_kv_g, ln_kv_b) @ Wkv.T
        q = q.reshape(B, Nq, H, HD).transpose(0, 2, 1, 3)
        kv = kv.reshape(B, Nk, 2, H, HD).transpose(2, 0, 3, 1, 4)
        k, v = (kv[0], kv[1])
        attn = jnp.einsum('bhqd,bhkd->bhqk', q, k) * scale
        attn = jax.nn.softmax(attn, axis=-1)
        out = jnp.einsum('bhqk,bhkd->bhqd', attn, v)
        out = out.transpose(0, 2, 1, 3).reshape(B, Nq, D)
        x = q_x + out @ Wo.T + bo
        h = jax.nn.silu(x @ W1.T + b1)
        x = x + h @ W2.T + b2
        return x

    def _L3_xattn_ref(query, key, value, Wq, bq, Wk, bk, Wv, bv, Wo, bo, gamma, beta):
        import jax, jax.numpy as jnp
        import numpy as np
        D_MODEL = 256
        NUM_HEADS = 16
        D_K = D_MODEL // NUM_HEADS
        BATCH = 4
        SEQ = 512

        def _layer_norm(x, gamma, beta, eps=1e-05):
            mu = jnp.mean(x, axis=-1, keepdims=True)
            var = jnp.var(x, axis=-1, keepdims=True)
            return (x - mu) * jax.lax.rsqrt(var + eps) * gamma + beta
        B, S, _ = query.shape
        residual = query
        Q = (query @ Wq + bq).reshape(B, S, NUM_HEADS, D_K).transpose(0, 2, 1, 3)
        K = (key @ Wk + bk).reshape(B, -1, NUM_HEADS, D_K).transpose(0, 2, 1, 3)
        V = (value @ Wv + bv).reshape(B, -1, NUM_HEADS, D_K).transpose(0, 2, 1, 3)
        scale = 1.0 / jnp.sqrt(jnp.asarray(D_K, query.dtype))
        scores = jnp.einsum('bhqd,bhkd->bhqk', Q, K) * scale
        attn = jax.nn.softmax(scores, axis=-1)
        ctx = jnp.einsum('bhqk,bhkd->bhqd', attn, V)
        ctx = ctx.transpose(0, 2, 1, 3).reshape(B, S, D_MODEL)
        out = ctx @ Wo + bo
        return _layer_norm(residual + out, gamma, beta)
    x = _L0_xattn_ref(x, ctx_1024, L0_xattn_swq, L0_xattn_sbq, L0_xattn_swk, L0_xattn_sbk, L0_xattn_swv, L0_xattn_sbv, L0_xattn_swo, L0_xattn_sbo, L0_xattn_cwq, L0_xattn_cbq, L0_xattn_cwk, L0_xattn_cbk, L0_xattn_cwv, L0_xattn_cbv, L0_xattn_cwo, L0_xattn_cbo, L0_xattn_w1, L0_xattn_b1, L0_xattn_w2, L0_xattn_b2, L0_xattn_g1, L0_xattn_be1, L0_xattn_g2, L0_xattn_be2, L0_xattn_g3, L0_xattn_be3)
    x = _L1_xattn_ref(x, ctx_1024, L1_xattn_sa_q_W, L1_xattn_sa_q_b, L1_xattn_sa_k_W, L1_xattn_sa_k_b, L1_xattn_sa_v_W, L1_xattn_sa_v_b, L1_xattn_ca_q_W, L1_xattn_ca_q_b, L1_xattn_ca_k_W, L1_xattn_ca_k_b, L1_xattn_ca_v_W, L1_xattn_ca_v_b, L1_xattn_m_Wq, L1_xattn_m_bq, L1_xattn_m_Wk, L1_xattn_m_bk, L1_xattn_m_Wv, L1_xattn_m_bv, L1_xattn_m_Wo, L1_xattn_m_bo, L1_xattn_c_Wq, L1_xattn_c_bq, L1_xattn_c_Wk, L1_xattn_c_bk, L1_xattn_c_Wv, L1_xattn_c_bv, L1_xattn_c_Wo, L1_xattn_c_bo, L1_xattn_ff_W1, L1_xattn_ff_b1, L1_xattn_ff_W2, L1_xattn_ff_b2, L1_xattn_ln1_g, L1_xattn_ln1_b, L1_xattn_ln2_g, L1_xattn_ln2_b, L1_xattn_ln3_g, L1_xattn_ln3_b)
    x = _L2_xattn_ref(x, ctx_1024, L2_xattn_Wq, L2_xattn_Wkv, L2_xattn_Wo, L2_xattn_bo, L2_xattn_ln_q_g, L2_xattn_ln_q_b, L2_xattn_ln_kv_g, L2_xattn_ln_kv_b, L2_xattn_W1, L2_xattn_b1, L2_xattn_W2, L2_xattn_b2)
    x = _L3_xattn_ref(x, ctx_1024, ctx_1024, L3_xattn_Wq, L3_xattn_bq, L3_xattn_Wk, L3_xattn_bk, L3_xattn_Wv, L3_xattn_bv, L3_xattn_Wo, L3_xattn_bo, L3_xattn_gamma, L3_xattn_beta)
    return x

_drawn_inputs = setup_inputs


def setup_inputs(seed=0):
    import zlib

    import numpy as np

    out = dict(_drawn_inputs(seed))
    spreads = {'L0_xattn_sbq': (0.0, 0.8),
     'L0_xattn_sbk': (0.0, 2.0),
     'L0_xattn_sbv': (0.0, 0.1),
     'L0_xattn_sbo': (0.0, 0.1),
     'L0_xattn_cbq': (0.0, 0.8),
     'L0_xattn_cbk': (0.0, 2.0),
     'L0_xattn_cbv': (0.0, 0.302),
     'L0_xattn_cbo': (0.0, 0.1),
     'L0_xattn_b1': (0.0, 0.1),
     'L0_xattn_b2': (0.0, 0.1),
     'L0_xattn_g1': (1.0, 0.2),
     'L0_xattn_be1': (0.0, 0.1),
     'L0_xattn_g2': (1.0, 0.2),
     'L0_xattn_be2': (0.0, 0.1),
     'L0_xattn_g3': (1.0, 0.2),
     'L0_xattn_be3': (0.0, 0.1),
     'L1_xattn_ln1_g': (1.0, 0.2),
     'L1_xattn_ln1_b': (0.0, 0.1),
     'L1_xattn_ln2_g': (1.0, 0.2),
     'L1_xattn_ln2_b': (0.0, 0.1),
     'L1_xattn_ln3_g': (1.0, 0.2),
     'L1_xattn_ln3_b': (0.0, 0.1),
     'L2_xattn_bo': (0.0, 0.1),
     'L2_xattn_ln_q_g': (1.0, 0.6),
     'L2_xattn_ln_q_b': (0.0, 2.0),
     'L2_xattn_ln_kv_g': (1.0, 0.6),
     'L2_xattn_ln_kv_b': (0.0, 0.8),
     'L2_xattn_b1': (0.0, 0.1),
     'L2_xattn_b2': (0.0, 0.1),
     'L3_xattn_bq': (0.0, 0.8),
     'L3_xattn_bk': (0.0, 2.0),
     'L3_xattn_bv': (0.0, 0.278),
     'L3_xattn_bo': (0.0, 0.1),
     'L3_xattn_gamma': (1.0, 0.2),
     'L3_xattn_beta': (0.0, 0.1)}
    factors = {'L0_xattn_swq': 8.0,
     'L0_xattn_swk': 8.0,
     'L0_xattn_cwq': 8.0,
     'L0_xattn_cwk': 8.0,
     'L1_xattn_sa_q_W': 8.0,
     'L1_xattn_sa_q_b': 8.0,
     'L1_xattn_sa_k_W': 8.0,
     'L1_xattn_sa_k_b': 64.0,
     'L1_xattn_sa_v_W': 7.205,
     'L1_xattn_sa_v_b': 8.0,
     'L1_xattn_ca_q_W': 8.0,
     'L1_xattn_ca_q_b': 8.0,
     'L1_xattn_ca_k_W': 8.0,
     'L1_xattn_ca_k_b': 64.0,
     'L1_xattn_ca_v_W': 3.549,
     'L1_xattn_ca_v_b': 8.0,
     'L1_xattn_m_Wq': 8.0,
     'L1_xattn_m_bq': 8.0,
     'L1_xattn_m_Wk': 8.0,
     'L1_xattn_m_bk': 64.0,
     'L1_xattn_m_Wv': 7.101,
     'L1_xattn_m_bv': 8.0,
     'L1_xattn_m_Wo': 5.803,
     'L1_xattn_m_bo': 12.652,
     'L1_xattn_c_Wq': 8.0,
     'L1_xattn_c_bq': 8.0,
     'L1_xattn_c_Wk': 8.0,
     'L1_xattn_c_bk': 64.0,
     'L1_xattn_c_Wv': 3.687,
     'L1_xattn_c_bv': 8.0,
     'L1_xattn_c_Wo': 3.35,
     'L1_xattn_c_bo': 3.424,
     'L1_xattn_ff_b1': 8.0,
     'L1_xattn_ff_b2': 3.215,
     'L2_xattn_Wq': 8.0,
     'L3_xattn_Wq': 8.0,
     'L3_xattn_Wk': 8.0}
    for name, (base, spread) in spreads.items():
        noise = np.random.default_rng([zlib.crc32(name.encode()), seed]).standard_normal(out[name].shape)
        drawn = base * np.exp(spread * noise) if base else spread * noise
        out[name] = jnp.asarray(drawn.astype(out[name].dtype))
    for name, factor in factors.items():
        out[name] = (out[name] * factor).astype(out[name].dtype)
    return out
```

```python
from contextlib import ExitStack

import concourse.bass as bass
from concourse import mybir
from concourse.alu_op_type import AluOpType as ALU

F32 = mybir.dt.float32
BF16 = mybir.dt.bfloat16
ACT = mybir.ActivationFunctionType
AX_X = mybir.AxisListType.X

P = 128
B, TOK, D, H, HD, FF = 8, 512, 256, 16, 16, 1024
KT = D // P
TT = TOK // P
FT = FF // P
WIN = 64
WCOL = P + WIN
PAIR = 2 * HD
RG = P // PAIR
EPS = 1e-5
STEP = TOK

FULL, CAUSAL, WINDOW = range(3)
ATT_KIND = [WINDOW, FULL, CAUSAL, FULL, FULL, FULL]
ATT_SCALE = [HD ** -0.5, HD ** -0.5, D ** -0.5, D ** -0.5, HD ** -0.5, HD ** -0.5]
ATT_KV = ["x", "ctx", "x", "ctx", "nctx", "ctx"]
SUBS = [("att", 0, 0), ("att", 1, 1), ("ffn", 0, 2), ("att", 2, 3), ("att", 3, 4), ("ffn", 1, 5),
        ("pre", 0, 6), ("att", 4, None), ("ffn", 2, None), ("att", 5, 7)]
TURNS = [s + 1 < len(SUBS) and SUBS[s + 1][0] != "pre" for s in range(len(SUBS))]
KV_NORM = 8
FFN_ACT = [ACT.Gelu, ACT.Gelu, ACT.Silu]

SQ = [f"{m}{a}" for a in range(6) for m in ("q", "k", "v", "o")]
FOLDS = [f"{m}{a}" for a in (2, 3) for m in ("q", "k", "v")]
SQ_LOADED = [n for n in SQ if n not in FOLDS]
COLS = ([(f"bq{a}", KT) for a in range(6)] + [(f"bk{a}", KT) for a in range(6)] + [(f"bv{a}", KT) for a in range(6)]
        + [(f"in_{n}", KT) for n in FOLDS] + [(f"b1_{f}", FT) for f in range(3)]
        + [(f"g{n}", KT) for n in range(9)] + [(f"b{n}", KT) for n in range(9)])
ROWS = [f"bo{a}" for a in range(6)] + [f"b2_{f}" for f in range(3)] + [f"g{n}" for n in (0, 1, 2, 3, 4, 5, 7)] \
    + [f"b{n}" for n in (0, 1, 2, 3, 4, 5, 7)]
TABLES = [("eye", P), ("hide_kq", P), ("hide_qk", P), ("whide_kq", WCOL), ("whide_qk", WCOL), ("slope_k", 4 * P),
          ("next_block", WCOL), ("slope_row", 4 * WCOL), ("ones3", P), ("pick", 2 * P), ("zeros", 2 * PAIR)]


def offsets(names):
    at, out = 0, {}
    for n, w in names:
        out[n] = (at, w)
        at += w
    return out, at


COL_AT, NCOL = offsets(COLS)
ROW_AT, NROW = offsets([(n, D) for n in ROWS])
TAB_AT, NTAB = offsets(TABLES)


class Signal:

    def __init__(self, sem, places):
        self.sem, self.places, self.n, self.seen = sem, places, 1, {}

    def open(self, eng):
        eng.drain().then_inc(self.sem, 1)

    def nth(self, base, n):
        return self.sem, base + (1 + n)

    def mark(self, name, by=1):
        self.n += by
        assert self.n < STEP and name not in self.seen, (name, self.n)
        self.seen[name] = self.n
        return self.sem, by

    def past(self, base, name):
        return self.sem, base + self.places.get(name, 1)

    def fill(self, eng):
        eng.drain().then_inc(self.sem, STEP + 1 - self.n)


def program(nc, places, x_rows, x_cols, c_rows, c_cols, squares, folds_a, folds_b, w1, w2, cols, rows, tables, eye32,
            parity, out):
    nc.disable_value_cache = True
    with ExitStack() as stack:
        def sb(name, shape, dt=F32):
            return stack.enter_context(nc.sbuf_tensor(name, shape, dt))

        def sem(name):
            return stack.enter_context(nc.semaphore(name))

        signals = {}

        def signal(name):
            signals[name] = Signal(sem(name), places.get(name, {}))
            return signals[name]

        sq = sb("sq", [P, len(SQ), KT, D])
        w1s = sb("w1s", [P, 3, KT, FF])
        w2s = sb("w2s", [P, 3, FT, D])
        col = sb("col", [P, NCOL])
        row = sb("row", [P, NROW])
        tab = sb("tab", [P, NTAB], BF16)
        eye = sb("eye", [P, P])
        par = sb("par", [P, 2])
        bqm = sb("bqm", [P, 6, KT, 2])
        m_half = sb("m_half", [P, TT])
        x = sb("x", [P, TT, D])
        y = sb("y", [P, TT, D])
        ctok = sb("ctok", [P, TT, D])
        xT = sb("xT", [P, KT, TOK])
        cT = sb("cT", [P, KT, TOK])
        ncT = sb("ncT", [P, KT, TOK])
        qm = sb("qm", [P, KT, 2, TOK])
        qb = sb("qb", [P, KT, 2, TOK], BF16)
        kf = sb("kf", [P, KT, TOK])
        kb = sb("kb", [P, KT, TOK], BF16)
        va = sb("va", [P, TT, H, 2 * PAIR])
        negm = [sb(f"negm{t}", [P, TT, P]) for t in range(KT)]
        mT = [sb(f"mT{t}", [P, TOK], BF16) for t in range(KT)]
        probs = sb("probs", [P, 2, RG, TOK])
        hid = probs[:].rearrange("p a r n -> p (a r) n")
        rec = sb("rec", [P, TOK])
        oT = xT
        st6 = sb("st6", [P, TT, 6])
        sm1 = sb("sm1", [P, 8, TT])

        st = stack.enter_context(nc.psum_tensor("st", [P, 4, TOK], F32))
        pv = stack.enter_context(nc.psum_tensor("pv", [P, 2, TOK], F32))
        sm = stack.enter_context(nc.psum_tensor("sm", [P, 2, TOK], F32))

        def cv(name):
            a, w = COL_AT[name]
            return col[:, a:a + w]

        def rv(name):
            a, w = ROW_AT[name]
            return row[:, a:a + w]

        def rows4(name):
            return rv(name).unsqueeze(1).to_broadcast([P, TT, D])

        def tb(name):
            a, w = TAB_AT[name]
            return tab[:, a:a + w]

        def sqw(name):
            return sq[:, SQ.index(name)]

        loaded = sem("loaded")
        fold_made = sem("fold_made")
        fold_kept = sem("fold_kept")
        prep = sem("prep")
        ready = sem("ready")
        pool_ready = sem("pool_ready")
        x_in = sem("x_in")
        xT_in = sem("xT_in")
        c_in = sem("c_in")
        cT_in = sem("cT_in")
        stored = sem("stored")
        st_filled = signal("st_filled")
        st_drained = signal("st_drained")
        sm_filled = signal("sm_filled")
        sm_drained = signal("sm_drained")
        probs_used = signal("probs_used")
        pv_filled = signal("pv_filled")
        heads_out = signal("heads_out")
        cast_made = signal("cast_made")
        row_step = signal("row_step")
        pool_step = signal("pool_step")

        N_WLOADS = 10
        FOLD_JOBS = len(FOLDS) * (KT + KT) + 5

        block = stack.enter_context(nc.Block())

        @block.sync
        def _(sp):
            fa = va[:].rearrange("p a h c -> p (a h c)")[:, 0:6 * KT * D]
            fb = hid.rearrange("p a n -> p (a n)")[:, 0:6 * KT * D]
            sp.dma_start(fa, folds_a).then_inc(loaded, 16)
            sp.dma_start(fb, folds_b).then_inc(loaded, 16)
            sp.dma_start(col[:], cols).then_inc(loaded, 16)
            sp.dma_start(row[:], rows).then_inc(loaded, 16)
            sp.dma_start(tab[:], tables).then_inc(loaded, 16)
            sp.dma_start(eye[:], eye32).then_inc(loaded, 16)
            sp.dma_start(par[:], parity).then_inc(loaded, 16)
            sp.dma_start(sq[:].rearrange("p s k n -> p (s k n)"), squares).then_inc(loaded, 16)
            sp.dma_start(w1s[:].rearrange("p f k n -> p (f k n)"), w1).then_inc(loaded, 16)
            sp.dma_start(w2s[:].rearrange("p f k n -> p (f k n)"), w2).then_inc(loaded, 16)


        @block.tensor
        def _(pe):
            fa = va[:].rearrange("p a h c -> p (a h c)")[:, 0:6 * KT * D].rearrange("p (j k n) -> p j k n", j=6, k=KT)
            fb = hid.rearrange("p a n -> p (a n)")[:, 0:6 * KT * D].rearrange("p (j k n) -> p j k n", j=6, k=KT)
            pe.wait_ge(loaded, 16 * N_WLOADS)
            job = 0

            def fold_bank(pe):
                if job >= 4:
                    pe.wait_ge(fold_kept, job - 3)
                return job % 4

            for j in range(len(FOLDS)):
                for t in range(KT):
                    b = fold_bank(pe)
                    for k in range(KT):
                        mm = pe.matmul(st[:, b, 0:D], fa[:, j, k, t * P:(t + 1) * P], fb[:, j, k, :],
                                       start=(k == 0), stop=(k == KT - 1))
                    mm.then_inc(fold_made, 1)
                    job += 1
                for t in range(KT):
                    b = fold_bank(pe)
                    for k in range(KT):
                        mm = pe.matmul(st[:, b, 0:1], fb[:, j, k, t * P:(t + 1) * P], cv(f"in_{FOLDS[j]}")[:, k:k + 1],
                                       start=(k == 0), stop=(k == KT - 1))
                    mm.then_inc(fold_made, 1)
                    job += 1
            for n, a in enumerate((0, 1, 2, 3, 5)):
                b = fold_bank(pe)
                pe.wait_ge(prep, 1 + n)
                for k in range(KT):
                    mm = pe.matmul(st[:, b, 0:D], qm[:, k, n % 2, 0:P], sqw(f"o{a}")[:, k, :],
                                   start=(k == 0), stop=(k == KT - 1))
                mm.then_inc(fold_made, 1)
                job += 1
            assert job == FOLD_JOBS
            pe.wait_ge(ready, 1)
            pe.wait_ge(pool_ready, 3)

            for sig in (st_filled, sm_filled, probs_used, pv_filled):
                sig.open(pe)

            with pe.Fori(0, B * TOK, TOK) as tok:
                jobs = {"st": 0, "sm": 0}

                def st_bank():
                    n = jobs["st"]
                    jobs["st"] += 1
                    pe.wait_ge(*st_drained.nth(tok, max(n - 3, 0)))
                    return n % 4

                def sm_bank():
                    n = jobs["sm"]
                    jobs["sm"] += 1
                    pe.wait_ge(*sm_drained.nth(tok, max(n - 1, 0)))
                    return n % 2

                def project(name, src, key):
                    for t in range(KT):
                        b = st_bank()
                        for k in range(KT):
                            mm = pe.matmul(st[:, b, :], sqw(name)[:, k, t * P:(t + 1) * P], src[:, k, :],
                                           start=(k == 0), stop=(k == KT - 1))
                        mm.then_inc(*st_filled.mark((key, t)))

                def max_unit(a, t, p, i):
                    kind = ATT_KIND[a]
                    k0 = max(0, i * P - WIN) if kind == WINDOW else 0
                    k1 = TOK if kind == FULL else (i + 1) * P
                    for r in range(RG):
                        b = sm_bank()
                        g = slice(32 * r, 32 * r + 32)
                        mm = pe.matmul(sm[:, b, 0:k1 - k0], qb[g, t, p, i * P:(i + 1) * P], kb[g, t, k0:k1],
                                       start=True, stop=(kind == FULL))
                        if kind == CAUSAL:
                            mm = pe.matmul(sm[:, b, i * P:k1], tb("eye"), tb("hide_qk"), start=False, stop=True)
                        if kind == WINDOW:
                            w = WCOL - (k1 - k0)
                            pe.matmul(sm[:, b, 0:k1 - k0], tb("eye"), tb("whide_qk")[:, w:WCOL], start=False, stop=False)
                            z = (2 * t + p) * WCOL
                            mm = pe.matmul(sm[:, b, 0:k1 - k0], tb("ones3")[g, :], tb("slope_row")[g, z + w:z + WCOL],
                                           start=False, stop=True)
                        mm.then_inc(*sm_filled.mark(("max", a, t, p, i, r)))

                def turn_max(a, t):
                    pe.wait_ge(*sm_drained.past(tok, ("max", a, t, 1, TT - 1, RG - 1)))
                    b = sm_bank()
                    for i in range(TT):
                        mm = pe.transpose(sm[:, b, i * P:(i + 1) * P], negm[t][:, i, :], eye[:])
                    mm.then_inc(*sm_filled.mark(("turn", a, t)))

                def span(a, k):
                    kind = ATT_KIND[a]
                    return (0, TOK) if kind == FULL else (k * P, TOK) if kind == CAUSAL else \
                        (k * P, min(TOK, k * P + WCOL))

                def scores(a, t, p, k):
                    kind = ATT_KIND[a]
                    q0, q1 = span(a, k)
                    n = q1 - q0
                    if p == 0 and k == 0:
                        pe.wait_ge(*sm_drained.past(tok, ("turn", a, t)))
                    for r in range(RG):
                        b = st_bank()
                        g = slice(32 * r, 32 * r + 32)
                        pe.matmul(st[:, b, 0:n], kf[g, t, k * P:(k + 1) * P], qm[g, t, p, q0:q1], start=True, stop=False)
                        mm = pe.matmul(st[:, b, 0:n], tb("pick")[g, p * P:(p + 1) * P], mT[t][g, q0:q1],
                                       start=False, stop=(kind == FULL))
                        if kind == CAUSAL:
                            mm = pe.matmul(st[:, b, 0:P], tb("eye"), tb("hide_kq"), start=False, stop=True)
                        if kind == WINDOW:
                            z = (2 * t + p) * P
                            pe.matmul(st[:, b, 0:n], tb("eye"), tb("whide_kq")[:, 0:n], start=False, stop=False)
                            mm = pe.matmul(st[:, b, 0:n], tb("slope_k")[g, z:z + P], tb("next_block")[g, 0:n],
                                           start=False, stop=True)
                        mm.then_inc(*st_filled.mark(("scores", a, t, p, k, r)))

                def values(a, t, p, k):
                    q0, q1 = span(a, k)
                    u = 4 * p + k
                    if u == 0:
                        if t == 0:
                            pe.wait_ge(*heads_out.nth(tok, 0)) if a == 0 else pe.wait_ge(*heads_out.past(tok, (a - 1, 1)))
                        else:
                            pe.wait_ge(*heads_out.past(tok, (a, 0)))
                        if ATT_KIND[a] == WINDOW:
                            for r in range(RG):
                                pe.matmul(pv[64 * (r % 2):64 * (r % 2) + 64, r // 2, :], tb("zeros"), tab[:, 0:TOK],
                                          start=True, stop=False)
                    for r in range(RG):
                        if r % 2 == 0:
                            pe.wait_ge(*st_drained.past(tok, ("probs", a, t, p, k, r // 2)))
                        mm = pe.matmul(pv[64 * (r % 2):64 * (r % 2) + 64, r // 2, q0:q1], va[:, k, 8 * t + 2 * r + p, :],
                                       probs[:, u % 2, r, 0:q1 - q0], 
                                       start=(u == 0 and ATT_KIND[a] != WINDOW), stop=(u == 7))
                    mm.then_inc(*probs_used.mark((a, t, p, k)))

                def attend(a, q_src):
                    kv = {"x": xT, "ctx": cT, "nctx": ncT}[ATT_KV[a]]
                    if a == 1:
                        pe.wait_ge(cT_in, (tok // 32) + 16)
                    project(f"k{a}", kv, ("k", a))
                    for k in range(TT):
                        b = st_bank()
                        for j in range(KT):
                            mm = pe.matmul(st[:, b, 0:D], kv[:, j, k * P:(k + 1) * P], sqw(f"v{a}")[:, j, :],
                                           start=(j == 0), stop=(j == KT - 1))
                        mm.then_inc(*st_filled.mark((("v", a), k)))
                    project(f"q{a}", q_src, ("q", a))
                    pe.wait_ge(*cast_made.past(tok, ("k", a)))
                    pe.wait_ge(*cast_made.past(tok, ("q", a)))
                    for p in range(2):
                        for i in range(TT):
                            max_unit(a, 0, p, i)
                    turn_max(a, 0)
                    for t in range(KT):
                        units = [(p, k) for p in range(2) for k in range(TT)]
                        for n, (p, k) in enumerate(units):
                            scores(a, t, p, k)
                            if t == 0:
                                max_unit(a, 1, p, k)
                            if n:
                                values(a, t, *units[n - 1])
                        values(a, t, *units[-1])
                        pe.drain().then_inc(*pv_filled.mark((a, t)))
                        if t == 0:
                            turn_max(a, 1)

                def rows_out(s, src, weight, n, waits):
                    for sig, name in waits:
                        pe.wait_ge(*sig.past(tok, name))
                    for i in range(TT):
                        b = sm_bank()
                        for j in range(n):
                            mm = pe.matmul(sm[:, b, 0:D], src[:, j, i * P:(i + 1) * P], weight[:, j, :],
                                           start=(j == 0), stop=(j == n - 1))
                        mm.then_inc(*sm_filled.mark(("rows", s, i)))

                def turn_rows(s, src, step):
                    pe.wait_ge(*row_step.past(tok, step))
                    for j in range(KT):
                        b = st_bank()
                        for i in range(TT):
                            mm = pe.transpose(st[:, b, i * P:(i + 1) * P], src[:, i, j * P:(j + 1) * P], eye[:])
                        mm.then_inc(*st_filled.mark(("turn", s, j)))

                pe.wait_ge(xT_in, (tok // 32) + 16)
                turn_rows("ctx", ctok, ("z", "ctx"))
                for s, (kind, n, norm) in enumerate(SUBS):
                    if s and TURNS[s - 1]:
                        pe.wait_ge(*st_drained.past(tok, ("turn", s - 1, KT - 1)))
                    if kind == "att":
                        attend(n, xT)
                        rows_out(s, oT, sqw(f"o{n}"), KT, [(heads_out, (n, 0)), (heads_out, (n, 1))])
                    elif kind == "ffn":
                        for f in range(FT):
                            b = st_bank()
                            for k in range(KT):
                                mm = pe.matmul(st[:, b, :], w1s[:, n, k, f * P:(f + 1) * P], xT[:, k, :],
                                               start=(k == 0), stop=(k == KT - 1))
                            mm.then_inc(*st_filled.mark(("hid", n, f)))
                        rows_out(s, hid, w2s[:, n], FT, [(st_drained, ("hid", n, FT - 1))])
                    if TURNS[s]:
                        turn_rows(s, y, ("z", s))
                for sig in (st_filled, sm_filled, probs_used, pv_filled):
                    sig.fill(pe)

        @block.scalar
        def _(act):
            act.wait_ge(ready, 1)
            act.wait_ge(pool_ready, 3)
            st_drained.open(act)
            with act.Fori(0, B) as batch:
                tok = batch * TOK
                rows_of = lambda a: a[bass.ds(batch, 1)].rearrange("o (t p) d -> p (o t) d", p=P)
                cols_of = lambda a: a[bass.ds(batch, 1)].rearrange("o (k p) n -> p (o k) n", p=P)
                for sig in (st_filled, pool_step, row_step):
                    act.wait_ge(*sig.nth(tok, 0))
                act.dma_start(xT[:], cols_of(x_cols)).then_inc(xT_in, 16)
                act.dma_start(x[:], rows_of(x_rows)).then_inc(x_in, 16)
                act.dma_start(cT[:], cols_of(c_cols)).then_inc(cT_in, 16)
                act.dma_start(ctok[:], rows_of(c_rows)).then_inc(c_in, 16)

                def turned(s, dst, norm):
                    for j in range(KT):
                        act.wait_ge(*st_filled.past(tok, ("turn", s, j)))
                        if norm is None:
                            i = act.activation(dst[:, j, :], st[:, jobs[0] % 4, :], ACT.Identity)
                        else:
                            i = act.activation(dst[:, j, :], st[:, jobs[0] % 4, :], ACT.Identity,
                                               bias=cv(f"b{norm}")[:, j:j + 1], scale=cv(f"g{norm}")[:, j:j + 1])
                        jobs[0] += 1
                        i.then_inc(*st_drained.mark(("turn", s, j)))

                jobs = [0]
                turned("ctx", ncT, KV_NORM)
                for s, (kind, n, norm) in enumerate(SUBS):
                    if kind == "att":
                        a = n
                        for t in range(KT):
                            act.wait_ge(*st_filled.past(tok, (("k", a), t)))
                            act.activation(kf[:, t, :], st[:, jobs[0] % 4, :], ACT.Identity,
                                           bias=cv(f"bk{a}")[:, t:t + 1]).then_inc(*st_drained.mark((("k", a), t)))
                            jobs[0] += 1
                        for k in range(TT):
                            act.wait_ge(*st_filled.past(tok, (("v", a), k)))
                            for p in range(2):
                                i = act.activation(
                                    va[:, k].rearrange("p (g e) c -> p g e c", e=2)[:, :, p, p * HD:(p + 1) * HD],
                                    st[:, jobs[0] % 4, 0:D].rearrange("p (g e c) -> p g e c", e=2, c=HD)[:, :, p, :],
                                    ACT.Identity)
                            i.then_inc(*st_drained.mark((("v", a), k)))
                            jobs[0] += 1
                        for t in range(KT):
                            act.wait_ge(*st_filled.past(tok, (("q", a), t)))
                            for p in range(2):
                                i = act.activation(qm[:, t, p, :], st[:, jobs[0] % 4, :], ACT.Identity,
                                                   bias=bqm[:, a, t, p:p + 1], scale=par[:, p:p + 1])
                            i.then_inc(*st_drained.mark((("q", a), t)))
                            jobs[0] += 1
                        last = None
                        for t in range(KT):
                            for p in range(2):
                                for k in range(TT):
                                    q0 = 0 if ATT_KIND[a] == FULL else k * P
                                    q1 = min(TOK, k * P + WCOL) if ATT_KIND[a] == WINDOW else TOK
                                    u = 4 * p + k
                                    units = [(t_, p_, k_) for t_ in range(KT) for p_ in range(2) for k_ in range(TT)]
                                    at = 8 * t + u
                                    if at >= 2:
                                        act.wait_ge(*probs_used.past(tok, (a, *units[at - 2])))
                                    for h in range(RG // 2):
                                        b = jobs[0] % 4
                                        act.wait_ge(*st_filled.past(tok, ("scores", a, t, p, k, 2 * h + 1)))
                                        act.activation(probs[:, u % 2, 2 * h:2 * h + 2, 0:q1 - q0],
                                                       st[:, b:b + 2, 0:q1 - q0], ACT.Exp, scale=ATT_SCALE[a]) \
                                            .then_inc(*st_drained.mark(("probs", a, t, p, k, h), 2))
                                        jobs[0] += 2
                    elif kind == "ffn":
                        for f in range(FT):
                            act.wait_ge(*st_filled.past(tok, ("hid", n, f)))
                            act.activation(hid[:, f, :], st[:, jobs[0] % 4, :], FFN_ACT[n],
                                           bias=cv(f"b1_{n}")[:, f:f + 1]).then_inc(*st_drained.mark(("hid", n, f)))
                            jobs[0] += 1
                    if TURNS[s]:
                        turned(s, xT, norm)
                act.wait_ge(*pool_step.past(tok, "out"))
                act.dma_start(rows_of(out), x[:]).then_inc(stored, 16)
                act.wait_ge(stored, batch * 16 + 16)
                st_drained.fill(act)

        @block.vector
        def _(dve):
            steps = [0]

            def prepared(ins):
                steps[0] += 1
                ins.then_inc(fold_kept, 1)

            dve.wait_ge(loaded, 16 * N_WLOADS)
            dve.wait_ge(pool_ready, 1)
            job = 0
            for j, name in enumerate(FOLDS):
                for t in range(KT):
                    dve.wait_ge(fold_made, job + 1)
                    dve.tensor_copy(sqw(name)[:, t, :], st[:, job % 4, 0:D]).then_inc(fold_kept, 1)
                    job += 1
                for t in range(KT):
                    b = cv(f"b{name}")[:, t:t + 1]
                    dve.wait_ge(fold_made, job + 1)
                    dve.tensor_tensor(b, st[:, job % 4, 0:1], b, ALU.add).then_inc(fold_kept, 1)
                    job += 1
            dve.wait_ge(fold_kept, job)
            for n, a in enumerate((0, 1, 2, 3, 5)):
                for k in range(KT):
                    ins = dve.tensor_scalar(qm[:, k, n % 2, 0:P], ones_(nc, rec, P), cv(f"bv{a}")[:, k:k + 1], None,
                                            ALU.mult)
                ins.then_inc(prep, 1)
                dve.wait_ge(fold_made, job + 1)
                dve.tensor_tensor(rv(f"bo{a}"), st[:, job % 4, 0:D], rv(f"bo{a}"), ALU.add).then_inc(fold_kept, 1)
                job += 1
            dve.wait_ge(fold_kept, job)
            after = [("b0", "bo1"), ("b1", "b2_0"), ("b2", "bo2"), ("b3", "bo3"), ("b4", "b2_1")]
            for b, extra in after:
                dve.tensor_tensor(rv(b), rv(b), rv(extra), ALU.add)
            for a in range(6):
                for p in range(2):
                    dve.tensor_scalar(bqm[:, a, :, p], cv(f"bq{a}"), par[:, p:p + 1], None, ALU.mult)
            dve.drain().then_inc(ready, 1)

            for sig in (sm_drained, heads_out, cast_made, row_step):
                sig.open(dve)
            with dve.Fori(0, B * TOK, TOK) as tok:
                smj = [0]

                def chain(ins, name):
                    ins.then_inc(*row_step.mark(name))
                    dve.wait_ge(*row_step.past(tok, name))

                def norm_rows(s, src, dst):
                    for i in range(TT):
                        ins = dve.bn_stats(st6[:, i, :], src[:, i, :])
                    chain(ins, ("stats", s))
                    e, o, me, mo = st6[:, :, 1], st6[:, :, 4], st6[:, :, 2], st6[:, :, 5]
                    dve.tensor_tensor(sm1[:, 0, :], e, o, ALU.add)
                    dve.tensor_tensor(sm1[:, 1, :], me, mo, ALU.add)
                    chain(dve.tensor_tensor(sm1[:, 2, :], e, o, ALU.subtract), ("halves", s))
                    dve.tensor_scalar(sm1[:, 3, :], sm1[:, 0, :], 0.5, None, ALU.mult)
                    chain(dve.tensor_tensor(sm1[:, 4, :], sm1[:, 2, :], sm1[:, 2, :], ALU.mult), ("sq", s))
                    chain(dve.scalar_tensor_tensor(sm1[:, 5, :], sm1[:, 4, :], float(D // 4), sm1[:, 1, :],
                                                   ALU.mult, ALU.add), ("var", s))
                    dve.tensor_scalar(sm1[:, 6, :], sm1[:, 5, :], 1.0 / D, EPS, ALU.mult, ALU.add) \
                        .then_inc(*row_step.mark(("eps", s)))
                    dve.wait_ge(*pool_step.past(tok, ("rstd", s)))
                    for i in range(TT):
                        ins = dve.tensor_scalar(dst[:, i, :], src[:, i, :], sm1[:, 3, i:i + 1], sm1[:, 7, i:i + 1],
                                                ALU.subtract, ALU.mult)
                    ins.then_inc(*row_step.mark(("z", s)))

                dve.wait_ge(c_in, (tok // 32) + 16)
                norm_rows("ctx", ctok, ctok)
                for s, (kind, n, norm) in enumerate(SUBS):
                    if kind == "att":
                        a = n
                        dve.wait_ge(*st_drained.past(tok, (("k", a), KT - 1)))
                        dve.tensor_copy(kb[:], kf[:]).then_inc(*cast_made.mark(("k", a)))
                        dve.wait_ge(*st_drained.past(tok, (("q", a), KT - 1)))
                        dve.tensor_copy(qb[:], qm[:]).then_inc(*cast_made.mark(("q", a)))
                        for t in range(KT):
                            for p in range(2):
                                for i in range(TT):
                                    kind_a = ATT_KIND[a]
                                    k0 = max(0, i * P - WIN) if kind_a == WINDOW else 0
                                    k1 = TOK if kind_a == FULL else (i + 1) * P
                                    for r in range(RG):
                                        dve.wait_ge(*sm_filled.past(tok, ("max", a, t, p, i, r)))
                                        dve.tensor_reduce(negm[t][:, i, 32 * r + p:32 * r + p + 1],
                                                          sm[:, smj[0] % 2, 0:k1 - k0], AX_X, ALU.max, negate=True) \
                                            .then_inc(*sm_drained.mark(("max", a, t, p, i, r)))
                                        smj[0] += 1
                            dve.wait_ge(*sm_filled.past(tok, ("turn", a, t)))
                            dve.tensor_copy(mT[t][:], sm[:, smj[0] % 2, :]).then_inc(*sm_drained.mark(("turn", a, t)))
                            smj[0] += 1
                        for t in range(KT):
                            dve.wait_ge(*pv_filled.past(tok, (a, t)))
                            for r in range(RG):
                                num = 64 * (r % 2)
                                ins = dve.reciprocal(rec[32 * r:32 * r + 32, :], pv[num + 32:num + 64, r // 2, :])
                            chain(ins, ("rec", a, t))
                            for r in range(RG):
                                num = 64 * (r % 2)
                                ins = dve.tensor_tensor(oT[32 * r:32 * r + 32, t, :], pv[num:num + 32, r // 2, :],
                                                        rec[32 * r:32 * r + 32, :], ALU.mult)
                            ins.then_inc(*heads_out.mark((a, t)))
                    if kind == "pre":
                        dve.wait_ge(*pool_step.past(tok, ("x", s - 1)))
                        norm_rows(s, x, y)
                        continue
                    dve.wait_ge(*pool_step.past(tok, ("x", s - 1)))
                    if kind == "att" and n == 0:
                        pass
                    for i in range(TT):
                        dve.wait_ge(*sm_filled.past(tok, ("rows", s, i)))
                        ins = dve.tensor_tensor(y[:, i, :], sm[:, smj[0] % 2, 0:D], x[:, i, :], ALU.add)
                        ins.then_inc(*sm_drained.mark(("rows", s, i)))
                        smj[0] += 1
                    dve.wait_ge(*sm_drained.past(tok, ("rows", s, TT - 1)))
                    if norm is None:
                        dve.tensor_copy(sm1[:, 0, :], sm1[:, 1, :]).then_inc(*row_step.mark(("z", s)))
                    else:
                        norm_rows(s, y, y)
                for sig in (sm_drained, heads_out, cast_made, row_step):
                    sig.fill(dve)

        @block.gpsimd
        def _(pool):
            nc.gpsimd.memset(rec[:], 1.0).then_inc(pool_ready, 1)
            nc.gpsimd.memset(m_half[:], -0.5)
            for t in range(KT):
                nc.gpsimd.memset(negm[t][:], 0.0)
            nc.gpsimd.memset(sm1[:], 0.0).then_inc(pool_ready, 1)
            pool.wait_ge(ready, 1)
            nc.gpsimd.memset(va[:], 0.0).then_inc(prep, 1)
            pool.wait_ge(prep, 6)
            for p in range(2):
                ins = nc.gpsimd.memset(va[:].rearrange("p k (g e) c -> p (k g) e c", e=2)
                                       [:, :, p, PAIR + p * HD:PAIR + (p + 1) * HD], 1.0)
            ins.then_inc(pool_ready, 1)
            pool.wait_ge(pool_ready, 3)

            pool_step.open(pool)
            with pool.Fori(0, B * TOK, TOK) as tok:
                def rstd(s):
                    pool.wait_ge(*row_step.past(tok, ("eps", s)))
                    pool.tensor_tensor(sm1[:, 7, :], sm1[:, 6, :], m_half[:], ALU.pow) \
                        .then_inc(*pool_step.mark(("rstd", s)))

                rstd("ctx")
                pool.wait_ge(x_in, (tok // 32) + 16)
                pool.tensor_tensor(x[:], x[:], rows4("bo0"), ALU.add).then_inc(*pool_step.mark(("x", -1)))
                for s, (kind, n, norm) in enumerate(SUBS):
                    if norm is not None:
                        rstd(s)
                    pool.wait_ge(*row_step.past(tok, ("z", s)))
                    if kind == "pre":
                        pool.tensor_tensor(x[:], x[:], rows4("bo4"), ALU.add).then_inc(*pool_step.mark(("x", s)))
                        continue
                    if norm is None:
                        pool.tensor_tensor(x[:], y[:], rows4("b2_2" if kind == "att" else "bo5"), ALU.add) \
                            .then_inc(*pool_step.mark(("x", s)))
                        continue
                    pool.tensor_tensor(x[:], y[:], rows4(f"g{norm}"), ALU.mult).then_inc(*pool_step.mark(("g", s)))
                    pool.wait_ge(*pool_step.past(tok, ("g", s)))
                    pool.tensor_tensor(x[:], x[:], rows4(f"b{norm}"), ALU.add) \
                        .then_inc(*pool_step.mark("out" if s == len(SUBS) - 1 else ("x", s)))
                pool_step.fill(pool)

    return {name: s.seen for name, s in signals.items()}


def ones_(nc, rec, n):
    return rec[:, 0:n]


def kernel(**inputs):
    import numpy as np
    import ml_dtypes
    import concourse.bacc as bacc
    from concourse.bass_utils import run_bass_kernel_spmd as run

    inp = {k: np.asarray(v) for k, v in inputs.items()}
    L0, L1, L2, L3 = (lambda n, l=l: inp[f"L{l}_xattn_{n}"] for l in range(4))

    def mat(w):
        k = w.shape[0] // P
        return w.reshape(k, P, w.shape[1]).transpose(1, 0, 2).reshape(P, -1)

    def colv(v):
        return v.reshape(-1, P).T

    def heads(w):
        return w.reshape(D, D).T

    zeros = np.zeros(D, np.float32)
    kv2 = L2("Wkv")
    square = {}
    for a, (l, pre) in {0: (L0, "s"), 1: (L0, "c")}.items():
        for m in "qkvo":
            square[f"{m}{a}"] = l(f"{pre}w{m}")
    for a, pre in ((2, "m"), (3, "c")):
        square[f"o{a}"] = L1(f"{pre}_Wo").T
        for m in "qkv":
            square[f"{m}{a}"] = np.zeros((D, D), np.float32)
    square.update(q4=L2("Wq").T, k4=kv2[:D].T, v4=kv2[D:].T, o4=L2("Wo").T)
    for m in "qkvo":
        square[f"{m}5"] = L3(f"W{m}")
    outer = {f"{m}{a}": heads(L1(f"{pre}_W{m}")) for a, pre in ((2, "m"), (3, "c")) for m in "qkv"}
    inner = {f"{m}{a}": L1(f"{pre}_{m}_W") for a, pre in ((2, "sa"), (3, "ca")) for m in "qkv"}

    vec = {}
    for a, l, names in ((0, L0, "sb{}"), (1, L0, "cb{}"), (5, L3, "b{}")):
        for m in "qkvo":
            vec[f"b{m}{a}"] = l(names.format(m))
    for a, pre, ipre in ((2, "m", "sa"), (3, "c", "ca")):
        for m in "qkv":
            vec[f"b{m}{a}"] = L1(f"{pre}_b{m}").reshape(D)
            vec[f"in_{m}{a}"] = L1(f"{ipre}_{m}_b")
        vec[f"bo{a}"] = L1(f"{pre}_bo")
    for m in "qkv":
        vec[f"b{m}4"] = zeros
    vec["bo4"] = L2("bo")
    vec.update(b1_0=L0("b1"), b1_1=L1("ff_b1"), b1_2=L2("b1"), b2_0=L0("b2"), b2_1=L1("ff_b2"), b2_2=L2("b2"))
    norms = [(L0("g1"), L0("be1")), (L0("g2"), L0("be2")), (L0("g3"), L0("be3")),
             (L1("ln1_g"), L1("ln1_b")), (L1("ln2_g"), L1("ln2_b")), (L1("ln3_g"), L1("ln3_b")),
             (L2("ln_q_g"), L2("ln_q_b")), (L3("gamma"), L3("beta")), (L2("ln_kv_g"), L2("ln_kv_b"))]
    for n, (g, b) in enumerate(norms):
        vec[f"g{n}"], vec[f"b{n}"] = g, b

    i, j = np.arange(P)[:, None], np.arange(P)[None, :]
    c = np.arange(WCOL)[None, :]
    hide = lambda m: np.where(m, np.float32(-1e30), np.float32(0))
    table = {
        "eye": np.eye(P), "hide_kq": hide(i > j), "hide_qk": hide(j > i),
        "whide_kq": hide(np.where(c < P, (i > c) | (c - i >= WIN), i <= c - P + WIN)),
        "whide_qk": hide(np.where(c < WIN, c <= i, (c - WIN > i) | (i - (c - WIN) >= WIN))),
        "ones3": np.broadcast_to((i % 32) < 3, (P, P)),
        "pick": np.concatenate([np.broadcast_to((i % 32) == p, (P, P)) for p in range(2)], 1),
        "zeros": np.zeros((P, 2 * PAIR)),
        "next_block": np.where(i % 32 < 3, 1, np.where(i % 32 < 6, c >= P, 0)),
    }

    def parts(v):
        out = []
        v = v.astype(np.float32)
        for _ in range(3):
            h = v.astype(ml_dtypes.bfloat16)
            out.append(h)
            v = v - h.astype(np.float32)
        return out

    slope_k = np.zeros((P, 4, P), ml_dtypes.bfloat16)
    slope_row = np.zeros((P, 4, WCOL), ml_dtypes.bfloat16)
    for h in range(H):
        t, r, p = h // 8, h % 8 // 2, h % 2
        slope = np.float32(2.0 ** (-8.0 * (h + 1) / H)) / np.float32(HD ** -0.5)
        for n in range(3):
            slope_k[32 * r + n, 2 * t + p] = parts(slope * np.arange(P))[n]
            slope_k[32 * r + 3 + n, 2 * t + p] = parts(np.full(P, -P * slope))[n]
            slope_row[32 * r + n, 2 * t + p] = parts(slope * (np.arange(WCOL) - WIN))[n]
    table["slope_k"], table["slope_row"] = slope_k.reshape(P, -1), slope_row.reshape(P, -1)

    def spread(v):
        return np.broadcast_to(v[None, :], (P, v.shape[0]))

    arrays = {
        "x_rows": inp["x"], "x_cols": inp["x"].transpose(0, 2, 1),
        "c_rows": inp["ctx_1024"], "c_cols": inp["ctx_1024"].transpose(0, 2, 1),
        "squares": np.concatenate([mat(square[n]) for n in SQ], 1),
        "folds_a": np.concatenate([mat(inner[n]) for n in FOLDS], 1),
        "folds_b": np.concatenate([mat(outer[n]) for n in FOLDS], 1),
        "w1": np.concatenate([mat(w) for w in (L0("w1"), L1("ff_W1").T, L2("W1").T)], 1),
        "w2": np.concatenate([mat(w) for w in (L0("w2"), L1("ff_W2").T, L2("W2").T)], 1),
        "cols": np.concatenate([colv(vec[n]) for n, _ in COLS], 1),
        "rows": np.concatenate([spread(vec[n]) for n in ROWS], 1),
        "tables": np.concatenate([np.asarray(table[n]).astype(ml_dtypes.bfloat16) for n, _ in TABLES], 1),
        "eye32": np.eye(P, dtype=np.float32),
        "parity": np.stack([(np.arange(P) // HD % 2 == p) for p in range(2)], 1).astype(np.float32),
    }
    arrays = {k: np.ascontiguousarray(v) for k, v in arrays.items()}

    def build(places):
        nc = bacc.Bacc("TRN2", target_bir_lowering=False, num_devices=1)
        args = [nc.dram_tensor(f"{k}_dram", v.shape, mybir.dt.from_np(v.dtype), kind="ExternalInput").ap()
                for k, v in arrays.items()]
        args.append(nc.dram_tensor("out_dram", (B, TOK, D), F32, kind="ExternalOutput").ap())
        return nc, program(nc, places, *args)

    _, places = build({})
    nc, _ = build(places)
    r = run(nc, [{f"{k}_dram": v for k, v in arrays.items()}], core_ids=[0])
    return r.results[0]["out_dram"]
```

```python
from contextlib import ExitStack

import concourse.bass as bass
from concourse import mybir
from concourse.alu_op_type import AluOpType as ALU

F32 = mybir.dt.float32
BF16 = mybir.dt.bfloat16
ACT = mybir.ActivationFunctionType
AX_X = mybir.AxisListType.X

P = 128
B, TOK, D, H, HD, FF = 8, 512, 256, 16, 16, 1024
KT = D // P
TT = TOK // P
FT = FF // P
WIN = 64
WCOL = P + WIN
HT = H // KT
PAIR = 2 * HD
GRP = 4
AHEAD = 2
EPS = 1e-5
STEP = TOK

FULL, CAUSAL, WINDOW = range(3)
ATT_KIND = [WINDOW, FULL, CAUSAL, FULL, FULL, FULL]
ATT_SCALE = [HD ** -0.5, HD ** -0.5, D ** -0.5, D ** -0.5, HD ** -0.5, HD ** -0.5]
ATT_KV = ["x", "ctx", "x", "ctx", "nctx", "ctx"]
SUBS = [("att", 0, 0), ("att", 1, 1), ("ffn", 0, 2), ("att", 2, 3), ("att", 3, 4), ("ffn", 1, 5),
        ("pre", 0, 6), ("att", 4, None), ("ffn", 2, None), ("att", 5, 7)]
TURNS = [s + 1 < len(SUBS) and SUBS[s + 1][0] != "pre" for s in range(len(SUBS))]
KV_NORM = 8


def sums_turn(h):
    return h // GRP - 1 if h >= GRP and h % GRP == 2 else None


def early_kv(s):
    return TURNS[s] and SUBS[s + 1][0] == "att" and ATT_KV[SUBS[s + 1][1]] != "x"


FFN_ACT = [ACT.Gelu, ACT.Gelu, ACT.Silu]

PART = {"k": {"h": (0, 1, 2), "m": (3, 4), "l": (5,)}, "q": {"h": (1, 3, 5), "m": (2, 4), "l": (0,)}}
MAXROW = 6 * HD
PLACE = {
    FULL: ([(k, 0, 0, TOK) for k in range(TT)], [(0, 2, TOK), (2, 2, TOK)]),
    CAUSAL: ([(0, 0, 0, TOK), (1, 0, P, TOK), (2, 0, 2 * P, TOK), (1, TOK - P, 3 * P, TOK)],
             [(0, 2, TOK), (2, 1, TOK // 2)]),
    WINDOW: ([(k // 2, k % 2 * 2 * P, k * P, min(TOK, (k + 2) * P)) for k in range(TT)],
             [(0, 1, TOK), (1, 1, 3 * P)]),
}

SQ = [f"{m}{a}" for a in range(6) for m in ("q", "k", "v", "o")]
FOLDS = [f"{m}{a}" for a in (2, 3) for m in ("q", "k", "v")]
SQ_LOADED = [n for n in SQ if n not in FOLDS]
COLS = ([(f"bv{a}", KT) for a in range(6)]
        + [(f"in_{n}", KT) for n in FOLDS] + [(f"b1_{f}", FT) for f in range(3)]
        + [(f"g{n}", KT) for n in range(9)] + [(f"b{n}", KT) for n in range(9)])
ROWS = [f"{m}{a}" for m in ("bq", "bk") for a in (0, 1, 2, 3, 5)] + [f"bo{a}" for a in range(6)] + [f"b2_{f}" for f in range(3)] + [f"g{n}" for n in (0, 1, 2, 3, 4, 5, 7)] \
    + [f"b{n}" for n in (0, 1, 2, 3, 4, 5, 7)]
TABLES = [("eye", P), ("hide_kq", P), ("hide_qk", P), ("whide_kq", 2 * P), ("whide_qk", WCOL), ("slope_k", 4 * P),
          ("next_block", 2 * P), ("slope_row", 4 * WCOL), ("ones3", P), ("zeros", PAIR)]


def offsets(names):
    at, out = 0, {}
    for n, w in names:
        out[n] = (at, w)
        at += w
    return out, at


COL_AT, NCOL = offsets(COLS)
ROW_AT, NROW = offsets([(n, D) for n in ROWS])
TAB_AT, NTAB = offsets(TABLES)


class Signal:

    def __init__(self, sem, places):
        self.sem, self.places, self.n, self.seen = sem, places, 1, {}

    def open(self, eng):
        eng.drain().then_inc(self.sem, 1)

    def nth(self, base, n):
        return self.sem, base + (1 + n)

    def mark(self, name, by=1):
        self.n += by
        assert self.n < STEP and name not in self.seen, (name, self.n)
        self.seen[name] = self.n
        return self.sem, by

    def past(self, base, name):
        return self.sem, base + self.places.get(name, 1)

    def fill(self, eng):
        eng.drain().then_inc(self.sem, STEP + 1 - self.n)


def program(nc, places, x_rows, x_cols, c_rows, c_cols, squares, folds_a, folds_b, w1, w2, cols, rows, tables, eye32,
            parity, out):
    nc.disable_value_cache = True
    with ExitStack() as stack:
        def sb(name, shape, dt=F32):
            return stack.enter_context(nc.sbuf_tensor(name, shape, dt))

        def sem(name):
            return stack.enter_context(nc.semaphore(name))

        signals = {}

        def signal(name):
            signals[name] = Signal(sem(name), places.get(name, {}))
            return signals[name]

        sq = sb("sq", [P, len(SQ), KT, D])
        w1s = sb("w1s", [P, KT, FF])
        w2s = sb("w2s", [P, FT, D])
        col = sb("col", [P, NCOL])
        row = sb("row", [P, NROW])
        tab = sb("tab", [P, NTAB], BF16)
        eye = sb("eye", [P, P])
        par = sb("par", [P, 2])
        m_half = sb("m_half", [P, TT])
        ones = sb("ones", [P, P])
        tokens = sb("tokens", [P, 3, TT, D])
        x, y, ctok = tokens[:, 0], tokens[:, 1], tokens[:, 2]
        xT = sb("xT", [P, KT, TOK])
        cT = sb("cT", [P, KT, TOK])
        ncT = sb("ncT", [P, KT, TOK])
        whole = {"k": ctok, "q": y}
        parts = {m: sb(f"{m}_parts", [P, TT, H, P], BF16) for m in "kq"}
        kb = sb("kb", [P, KT, TOK], BF16)
        qb = sb("qb", [P, 2, KT, TOK], BF16)
        turned_parts = sb("turned_parts", [P, 2, 2, TOK], BF16)
        va = sb("va", [P, TT, H, PAIR])
        probs = sb("probs", [P, 2, 4, TOK])
        hid = probs[:].rearrange("p a r n -> p (a r) n")
        rec = sb("rec", [P, TT, GRP])
        sums = oT = xT
        st6 = sb("st6", [P, TT, 6])
        sm1 = sb("sm1", [P, 8, TT])

        st = stack.enter_context(nc.psum_tensor("st", [P, 2, 2, TOK], F32))
        pv = stack.enter_context(nc.psum_tensor("pv", [P, TOK], F32))
        tr = stack.enter_context(nc.psum_tensor("tr", [P, 2, TOK], BF16))
        sm = stack.enter_context(nc.psum_tensor("sm", [P, 2, TOK], F32))

        def cv(name):
            a, w = COL_AT[name]
            return col[:, a:a + w]

        def rv(name):
            a, w = ROW_AT[name]
            return row[:, a:a + w]

        def rows_n(name, n):
            return rv(name).unsqueeze(1).to_broadcast([P, n, D])

        def tb(name):
            a, w = TAB_AT[name]
            return tab[:, a:a + w]

        def sqw(name):
            return sq[:, SQ.index(name)]

        def part(m, which):
            g = PART[m][which]
            step = g[1] - g[0] if len(g) > 1 else 1
            rows6 = parts[m][:, :, :, 0:MAXROW].rearrange("p i h (g c) -> p (i h) g c", c=HD)
            return rows6[:, :, g[0]:g[-1] + 1:step, :]

        def in_heads(rows):
            return rows.rearrange("p i (h c) -> p (i h) c", c=HD)

        loaded = sem("loaded")
        fold_made = sem("fold_made")
        fold_kept = sem("fold_kept")
        spread = sem("spread")
        ready = sem("ready")
        pool_ready = sem("pool_ready")
        x_in = sem("x_in")
        xT_in = sem("xT_in")
        c_in = sem("c_in")
        cT_in = sem("cT_in")
        w_in = [sem(f"w{f}_in") for f in range(3)]
        stored = sem("stored")
        st_filled = signal("st_filled")
        st_drained = signal("st_drained")
        sm_filled = signal("sm_filled")
        sm_drained = signal("sm_drained")
        tr_filled = signal("tr_filled")
        tr_drained = signal("tr_drained")
        head_done = signal("head_done")
        sums_kept = signal("sums_kept")
        split = signal("split")
        row_step = signal("row_step")
        pool_step = signal("pool_step")

        N_LOADS = 8
        BIASES = [(f"in_{n}", n, f"b{n}") for n in FOLDS if n[0] != "v"] \
            + [(f"bv{a}", f"o{a}", f"bo{a}") for a in (0, 1, 2, 3, 5)]
        FOLD_JOBS = len(FOLDS) * KT + 2 * KT

        block = stack.enter_context(nc.Block())

        @block.sync
        def _(sp):
            sp.dma_start(tokens[:].rearrange("p a t d -> p (a t d)"), folds_a).then_inc(loaded, 16)
            sp.dma_start(hid.rearrange("p a n -> p (a n)")[:, 0:6 * KT * D], folds_b).then_inc(loaded, 16)
            sp.dma_start(col[:], cols).then_inc(loaded, 16)
            sp.dma_start(row[:], rows).then_inc(loaded, 16)
            sp.dma_start(tab[:], tables).then_inc(loaded, 16)
            sp.dma_start(eye[:], eye32).then_inc(loaded, 16)
            sp.dma_start(par[:], parity).then_inc(loaded, 16)
            sp.dma_start(sq[:].rearrange("p s k n -> p (s k n)"), squares).then_inc(loaded, 16)

        @block.tensor
        def _(pe):
            fa = tokens[:].rearrange("p a t d -> p (a t d)").rearrange("p (j k n) -> p j k n", j=6, k=KT)
            fb = hid.rearrange("p a n -> p (a n)")[:, 0:6 * KT * D].rearrange("p (j k n) -> p j k n", j=6, k=KT)
            pe.wait_ge(loaded, 16 * N_LOADS)
            job = 0

            def fold_bank(pe):
                if job >= 4:
                    pe.wait_ge(fold_kept, job - 3)
                return st[:, job // 2 % 2, job % 2]

            for j, name in enumerate(FOLDS):
                for t in range(KT):
                    b = fold_bank(pe)
                    for k in range(KT):
                        mm = pe.matmul(b[:, 0:D], fa[:, j, k, t * P:(t + 1) * P], fb[:, j, k, :],
                                       start=(k == 0), stop=(k == KT - 1))
                    mm.then_inc(fold_made, 1)
                    job += 1
                for t in range(KT if name[0] == "v" else 0):
                    b = fold_bank(pe)
                    for k in range(KT):
                        mm = pe.matmul(b[:, 0:1], fb[:, j, k, t * P:(t + 1) * P], cv(f"in_{name}")[:, k:k + 1],
                                       start=(k == 0), stop=(k == KT - 1))
                    mm.then_inc(fold_made, 1)
                    job += 1
            assert job == FOLD_JOBS
            for n, (_, w, _) in enumerate(BIASES):
                b = fold_bank(pe)
                pe.wait_ge(spread, 1 + n)
                for k in range(KT):
                    mm = pe.matmul(b[:, 0:D], xT[:, k, n % 2 * P:(n % 2 + 1) * P],
                                   sqw(w)[:, k, :] if w[0] == "o" else fb[:, FOLDS.index(w), k, :],
                                   start=(k == 0), stop=(k == KT - 1))
                mm.then_inc(fold_made, 1)
                job += 1
            pe.wait_ge(ready, 1)
            pe.wait_ge(pool_ready, 2)

            for sig in (st_filled, sm_filled, tr_filled, head_done):
                sig.open(pe)

            with pe.Fori(0, B * TOK, TOK) as tok:
                jobs = {"st": 0, "sm": 0, "tr": 0, "group": 0}

                def st_pair():
                    n = jobs["st"]
                    jobs["st"] += 1
                    pe.wait_ge(*st_drained.nth(tok, max(n - 1, 0)))
                    return st[:, n % 2]

                def sm_bank():
                    n = jobs["sm"]
                    jobs["sm"] += 1
                    pe.wait_ge(*sm_drained.nth(tok, max(n - 1, 0)))
                    return sm[:, n % 2]

                def tr_bank():
                    pe.wait_ge(*tr_drained.nth(tok, jobs["tr"]))
                    jobs["tr"] += 1
                    return tr

                def turn_tiles(src):
                    pair = st_pair()
                    for j in range(KT):
                        for i in range(TT):
                            mm = pe.transpose(pair[:, j, i * P:(i + 1) * P], src[:, i, j * P:(j + 1) * P], eye[:])
                    return mm

                def project(m, a, src):
                    pair = st_pair() if m == "v" else None
                    for half in range(2):
                        b = pair[:, half] if m == "v" else sm_bank()
                        for i in range(2):
                            n = 2 * half + i
                            for j in range(KT):
                                mm = pe.matmul(b[:, i * D:(i + 1) * D], src[:, j, n * P:(n + 1) * P],
                                               sqw(f"{m}{a}")[:, j, :], start=(j == 0), stop=(j == KT - 1))
                        if m != "v":
                            mm.then_inc(*sm_filled.mark((m, a, half)))
                    if m == "v":
                        mm.then_inc(*st_filled.mark((m, a)))

                def keys_values(a):
                    if a == 1:
                        pe.wait_ge(cT_in, (tok // 32) + 16)
                    kv = {"x": xT, "ctx": cT, "nctx": ncT}[ATT_KV[a]]
                    project("k", a, kv)
                    project("v", a, kv)

                def turn_high(m, a):
                    pe.wait_ge(*sm_drained.past(tok, (m, a, 1)))
                    turn_tiles(whole[m]).then_inc(*st_filled.mark(("high", m, a)))

                def max_unit(a, h, i):
                    kind = ATT_KIND[a]
                    if (h, i) == (0, 0):
                        pe.wait_ge(*st_drained.past(tok, ("high", "q", a)))
                    k0 = max(0, i * P - WIN) if kind == WINDOW else 0
                    k1 = TOK if kind == FULL else (i + 1) * P
                    t, p = h // HT, h % 2
                    g = slice(h % HT // 2 * PAIR, (h % HT // 2 + 1) * PAIR)
                    b = sm_bank()
                    mm = pe.matmul(b[:, 0:k1 - k0], qb[g, p, t, i * P:(i + 1) * P], kb[g, t, k0:k1],
                                   start=True, stop=(kind == FULL))
                    if kind == CAUSAL:
                        mm = pe.matmul(b[:, i * P:k1], tb("eye"), tb("hide_qk"), start=False, stop=True)
                    if kind == WINDOW:
                        w = WCOL - (k1 - k0)
                        pe.matmul(b[:, 0:k1 - k0], tb("eye"), tb("whide_qk")[:, w:WCOL], start=False, stop=False)
                        z = (2 * t + p) * WCOL
                        mm = pe.matmul(b[:, 0:k1 - k0], tb("ones3")[g, :], tb("slope_row")[g, z + w:z + WCOL],
                                       start=False, stop=True)
                    mm.then_inc(*sm_filled.mark(("max", a, h, i)))

                def turn_parts(a, h):
                    pe.wait_ge(*sm_drained.past(tok, ("max", a, h, TT - 1)))
                    if h == 0:
                        pe.wait_ge(*row_step.past(tok, ("l", "q", a)))
                    b = tr_bank()
                    for m in range(2):
                        for i in range(TT):
                            mm = pe.transpose(b[:, m, i * P:(i + 1) * P], parts["kq"[m]][:, i, h, :], tb("eye"))
                    mm.then_inc(*tr_filled.mark(("parts", a, h)))

                def scores(a, h, e):
                    kind = ATT_KIND[a]
                    if e == 0:
                        pe.wait_ge(*tr_drained.past(tok, ("parts", a, h)))
                    t, p = h // HT, h % 2
                    g = slice(h % HT // 2 * PAIR, (h % HT // 2 + 1) * PAIR)
                    kk, qq = turned_parts[:, h % 2, 0], turned_parts[:, h % 2, 1]
                    pair = st_pair()
                    for k, (bank, c, q0, q1) in enumerate(PLACE[kind][0]):
                        if bank // 2 != e:
                            continue
                        n = q1 - q0
                        b = pair[:, bank % 2]
                        mm = pe.matmul(b[:, c:c + n], kk[:, k * P:(k + 1) * P], qq[:, q0:q1], start=True,
                                       stop=(kind == FULL))
                        if kind == CAUSAL:
                            mm = pe.matmul(b[:, c:c + P], tb("eye"), tb("hide_kq"), start=False, stop=True)
                        if kind == WINDOW:
                            z = (2 * t + p) * P
                            pe.matmul(b[:, c:c + n], tb("eye"), tb("whide_kq")[:, 0:n], start=False, stop=False)
                            mm = pe.matmul(b[:, c:c + n], tb("slope_k")[g, z:z + P], tb("next_block")[g, 0:n],
                                           start=False, stop=True)
                    mm.then_inc(*st_filled.mark(("scores", a, h, e)))

                def values(a, h, k):
                    kind = ATT_KIND[a]
                    j = h % GRP * PAIR
                    if k == 0:
                        pe.wait_ge(*st_drained.past(tok, ("probs", a, h, PLACE[kind][1][-1][0])))
                        if h % GRP == 0:
                            pe.wait_ge(*sums_kept.nth(tok, jobs["group"]))
                            jobs["group"] += 1
                        if kind == WINDOW:
                            pe.matmul(pv[j:j + PAIR, :], tb("zeros"), tab[:, 0:TOK], start=True, stop=False)
                    bank, c, q0, q1 = PLACE[kind][0][k]
                    mm = pe.matmul(pv[j:j + PAIR, q0:q1], va[:, k, h, :], probs[:, h % 2, bank, c:c + q1 - q0],
                                   start=(k == 0 and kind != WINDOW), stop=(k == TT - 1))
                    if k == TT - 1:
                        mm.then_inc(*head_done.mark((a, h)))

                def turn_sums(a, g):
                    pe.wait_ge(*sums_kept.past(tok, (a, g)))
                    b = sm_bank()
                    for i in range(TT):
                        mm = pe.transpose(b[:, i * P:(i + 1) * P], sums[:, g % 2, i * P:(i + 1) * P], eye[:])
                    mm.then_inc(*sm_filled.mark(("out", a, g)))

                def attend(a):
                    if ATT_KV[a] == "x":
                        keys_values(a)
                        turn_high("k", a)
                    project("q", a, xT)
                    turn_high("q", a)
                    for h in range(AHEAD):
                        for i in range(TT):
                            max_unit(a, h, i)
                    turn_parts(a, 0)
                    for h in range(H):
                        ahead = h + AHEAD < H
                        scores(a, h, 0)
                        if ahead:
                            max_unit(a, h + AHEAD, 0)
                            max_unit(a, h + AHEAD, 1)
                        if sums_turn(h) is not None:
                            turn_sums(a, sums_turn(h))
                        if ATT_KIND[a] != WINDOW:
                            scores(a, h, 1)
                        if h + 1 < H:
                            turn_parts(a, h + 1)
                        if h:
                            values(a, h - 1, 0)
                            values(a, h - 1, 1)
                        if ahead:
                            max_unit(a, h + AHEAD, 2)
                        if h:
                            values(a, h - 1, 2)
                            values(a, h - 1, 3)
                        if ahead:
                            max_unit(a, h + AHEAD, 3)
                    for i in range(TT):
                        values(a, H - 1, i)
                    turn_sums(a, H // GRP - 1)
                    pair = st_pair()
                    for t in range(KT):
                        pe.wait_ge(*sm_drained.past(tok, ("out", a, (t + 1) * HT // GRP - 1)))
                        for i in range(TT):
                            mm = pe.transpose(pair[:, t, i * P:(i + 1) * P], y[:, i, t * P:(t + 1) * P], eye[:])
                    mm.then_inc(*st_filled.mark(("oT", a)))

                def rows_out(s, src, weight, n):
                    for i in range(TT):
                        b = sm_bank()
                        for j in range(n):
                            mm = pe.matmul(b[:, 0:D], src[:, j, i * P:(i + 1) * P], weight[:, j, :],
                                           start=(j == 0), stop=(j == n - 1))
                        mm.then_inc(*sm_filled.mark(("rows", s, i)))

                def turn_rows(s, src, sig, step):
                    pe.wait_ge(*sig.past(tok, step))
                    turn_tiles(src).then_inc(*st_filled.mark(("turn", s)))

                pe.wait_ge(xT_in, (tok // 32) + 16)
                turn_rows("ctx", ctok, row_step, ("z", "ctx"))
                for s, (kind, n, norm) in enumerate(SUBS):
                    if s and TURNS[s - 1]:
                        pe.wait_ge(*st_drained.past(tok, ("turn", s - 1)))
                    if kind == "att":
                        attend(n)
                        pe.wait_ge(*st_drained.past(tok, ("oT", n)))
                        rows_out(s, oT, sqw(f"o{n}"), KT)
                    elif kind == "ffn":
                        pe.wait_ge(w_in[n], (tok // 16) + 32)
                        for f in range(FT // 2):
                            pair = st_pair()
                            for e in range(2):
                                for k in range(KT):
                                    mm = pe.matmul(pair[:, e], w1s[:, k, (2 * f + e) * P:(2 * f + e + 1) * P], xT[:, k, :],
                                                   start=(k == 0), stop=(k == KT - 1))
                            mm.then_inc(*st_filled.mark(("hid", n, f)))
                        pe.wait_ge(*st_drained.past(tok, ("hid", n, FT // 2 - 1)))
                        rows_out(s, hid, w2s, FT)
                    if TURNS[s]:
                        if early_kv(s):
                            keys_values(SUBS[s + 1][1])
                        if norm is None:
                            turn_rows(s, y, sm_drained, ("rows", s, TT - 1))
                        else:
                            turn_rows(s, y, row_step, ("z", s))
                        if early_kv(s):
                            turn_high("k", SUBS[s + 1][1])
                for sig in (st_filled, sm_filled, tr_filled, head_done):
                    sig.fill(pe)

        @block.scalar
        def _(act):
            act.wait_ge(ready, 1)
            act.wait_ge(pool_ready, 2)
            for sig in (st_drained, tr_drained, split, sums_kept):
                sig.open(act)
            with act.Fori(0, B) as batch:
                tok = batch * TOK
                rows_of = lambda a: a[bass.ds(batch, 1)].rearrange("o (t p) d -> p (o t) d", p=P)
                cols_of = lambda a: a[bass.ds(batch, 1)].rearrange("o (k p) n -> p (o k) n", p=P)
                jobs = {"st": 0}

                def pair_of():
                    jobs["st"] += 1
                    return st[:, (jobs["st"] - 1) % 2]

                def load_weights(f):
                    act.dma_start(w1s[:].rearrange("p k n -> p (k n)"), w1[:, f * KT * FF:(f + 1) * KT * FF]) \
                        .then_inc(w_in[f], 16)
                    act.dma_start(w2s[:].rearrange("p k n -> p (k n)"), w2[:, f * FT * D:(f + 1) * FT * D]) \
                        .then_inc(w_in[f], 16)

                def turned(s, dst, norm):
                    act.wait_ge(*st_filled.past(tok, ("turn", s)))
                    pair = pair_of()
                    for j in range(KT):
                        if norm is None:
                            i = act.activation(dst[:, j, :], pair[:, j], ACT.Identity)
                        else:
                            i = act.activation(dst[:, j, :], pair[:, j], ACT.Identity,
                                               bias=cv(f"b{norm}")[:, j:j + 1], scale=cv(f"g{norm}")[:, j:j + 1])
                    i.then_inc(*st_drained.mark(("turn", s)))

                def split_part(m, a, which):
                    if which == "h":
                        act.wait_ge(*sm_drained.past(tok, (m, a, 1)))
                    else:
                        act.wait_ge(*row_step.past(tok, ("rest", m, a)))
                    dst = part(m, which)
                    act.activation(dst, in_heads(whole[m]).unsqueeze(2).to_broadcast(list(dst.shape)), ACT.Identity) \
                        .then_inc(*split.mark((which, m, a)))

                def values_kept(a):
                    act.wait_ge(*st_filled.past(tok, ("v", a)))
                    pair = pair_of()
                    act.activation(va[:, :, :, 0:HD].rearrange("p i h c -> p (i h) c"),
                                   pair.rearrange("p b (i h c) -> p (b i h) c", i=2, c=HD), ACT.Identity) \
                        .then_inc(*st_drained.mark(("v", a)))

                def keys_split(a):
                    act.wait_ge(*st_filled.past(tok, ("high", "k", a)))
                    act.activation(kb[:], pair_of(), ACT.Identity).then_inc(*st_drained.mark(("high", "k", a)))
                    split_part("k", a, "h")
                    split_part("k", a, "m")

                def attend(a):
                    if ATT_KV[a] == "x":
                        values_kept(a)
                        keys_split(a)
                    act.wait_ge(*st_filled.past(tok, ("high", "q", a)))
                    pair = pair_of()
                    for p in range(2):
                        i = act.activation(qb[:, p], pair, ACT.Identity, scale=par[:, p:p + 1])
                    i.then_inc(*st_drained.mark(("high", "q", a)))
                    split_part("q", a, "h")
                    split_part("q", a, "m")

                    def parts_kept(h):
                        act.wait_ge(*tr_filled.past(tok, ("parts", a, h)))
                        act.activation(turned_parts[:, h % 2], tr[:], ACT.Identity) \
                            .then_inc(*tr_drained.mark(("parts", a, h)))

                    def keep_sums(g):
                        act.wait_ge(*head_done.past(tok, (a, (g + 1) * GRP - 1)))
                        if g >= 2:
                            act.wait_ge(*sm_filled.past(tok, ("out", a, g - 2)))
                        act.activation(sums[:, g % 2, :], pv[:], ACT.Identity).then_inc(*sums_kept.mark((a, g)))

                    parts_kept(0)
                    for h in range(H):
                        if h >= 2:
                            act.wait_ge(*head_done.past(tok, (a, h - 2)))
                        for bank, nb, n in PLACE[ATT_KIND[a]][1]:
                            if bank % 2 == 0:
                                act.wait_ge(*st_filled.past(tok, ("scores", a, h, bank // 2)))
                                pair = pair_of()
                            i = act.activation(probs[:, h % 2, bank:bank + nb, 0:n],
                                               pair[:, bank % 2:bank % 2 + nb, 0:n], ACT.Exp, scale=ATT_SCALE[a])
                            if ATT_KIND[a] != WINDOW or bank == 1:
                                i.then_inc(*st_drained.mark(("probs", a, h, bank)))
                        if h + 1 < H:
                            parts_kept(h + 1)
                        if h and h % GRP == 0:
                            keep_sums(h // GRP - 1)
                    keep_sums(H // GRP - 1)
                    act.wait_ge(*st_filled.past(tok, ("oT", a)))
                    act.activation(oT[:], pair_of(), ACT.Identity).then_inc(*st_drained.mark(("oT", a)))

                for sig in (st_filled, sm_filled, pool_step, row_step):
                    act.wait_ge(*sig.nth(tok, 0))
                act.dma_start(xT[:], cols_of(x_cols)).then_inc(xT_in, 16)
                act.dma_start(x, rows_of(x_rows)).then_inc(x_in, 16)
                act.dma_start(ctok, rows_of(c_rows)).then_inc(c_in, 16)
                act.dma_start(cT[:], cols_of(c_cols)).then_inc(cT_in, 16)
                load_weights(0)
                turned("ctx", ncT, KV_NORM)
                for s, (kind, n, norm) in enumerate(SUBS):
                    if kind == "att":
                        attend(n)
                    elif kind == "ffn":
                        for f in range(FT // 2):
                            act.wait_ge(*st_filled.past(tok, ("hid", n, f)))
                            pair = pair_of()
                            for e in range(2):
                                g = 2 * f + e
                                i = act.activation(hid[:, g, :], pair[:, e], FFN_ACT[n], bias=cv(f"b1_{n}")[:, g:g + 1])
                            i.then_inc(*st_drained.mark(("hid", n, f)))
                        if n + 1 < 3:
                            act.wait_ge(*sm_filled.past(tok, ("rows", s, TT - 1)))
                            load_weights(n + 1)
                    if TURNS[s]:
                        if early_kv(s):
                            values_kept(SUBS[s + 1][1])
                        turned(s, xT, norm)
                        if early_kv(s):
                            keys_split(SUBS[s + 1][1])
                act.wait_ge(*pool_step.past(tok, "out"))
                act.dma_start(rows_of(out), x).then_inc(stored, 16)
                act.wait_ge(stored, batch * 16 + 16)
                for sig in (st_drained, tr_drained, split, sums_kept):
                    sig.fill(act)

        @block.vector
        def _(dve):
            dve.wait_ge(loaded, 16 * N_LOADS)
            dve.wait_ge(pool_ready, 1)
            job = 0

            def fold_bank():
                dve.wait_ge(fold_made, job + 1)
                return st[:, job // 2 % 2, job % 2]

            for name in FOLDS:
                for t in range(KT):
                    dve.tensor_copy(sqw(name)[:, t, :], fold_bank()[:, 0:D]).then_inc(fold_kept, 1)
                    job += 1
                for t in range(KT if name[0] == "v" else 0):
                    b = cv(f"b{name}")[:, t:t + 1]
                    dve.tensor_tensor(b, fold_bank()[:, 0:1], b, ALU.add).then_inc(fold_kept, 1)
                    job += 1
            dve.wait_ge(fold_kept, job)
            for n, (c, _, to) in enumerate(BIASES):
                for k in range(KT):
                    ins = dve.tensor_scalar(xT[:, k, n % 2 * P:(n % 2 + 1) * P], ones[:], cv(c)[:, k:k + 1], None, ALU.mult)
                ins.then_inc(spread, 1)
                dve.tensor_tensor(rv(to), fold_bank()[:, 0:D], rv(to), ALU.add).then_inc(fold_kept, 1)
                job += 1
            dve.wait_ge(fold_kept, job)
            for b, extra in [("b0", "bo1"), ("b1", "b2_0"), ("b2", "bo2"), ("b3", "bo3"), ("b4", "b2_1")]:
                dve.tensor_tensor(rv(b), rv(b), rv(extra), ALU.add)
            dve.drain().then_inc(ready, 1)

            for sig in (sm_drained, row_step):
                sig.open(dve)
            with dve.Fori(0, B * TOK, TOK) as tok:
                jobs = {"sm": 0}

                def sm_bank():
                    jobs["sm"] += 1
                    return sm[:, (jobs["sm"] - 1) % 2]

                def chain(ins, name):
                    ins.then_inc(*row_step.mark(name))
                    dve.wait_ge(*row_step.past(tok, name))

                def norm_rows(s, src, dst):
                    for i in range(TT):
                        ins = dve.bn_stats(st6[:, i, :], src[:, i, :])
                    chain(ins, ("stats", s))
                    e, o, me, mo = st6[:, :, 1], st6[:, :, 4], st6[:, :, 2], st6[:, :, 5]
                    dve.tensor_tensor(sm1[:, 0, :], e, o, ALU.add)
                    dve.tensor_tensor(sm1[:, 1, :], me, mo, ALU.add)
                    chain(dve.tensor_tensor(sm1[:, 2, :], e, o, ALU.subtract), ("halves", s))
                    dve.tensor_scalar(sm1[:, 3, :], sm1[:, 0, :], 0.5, None, ALU.mult)
                    chain(dve.tensor_tensor(sm1[:, 4, :], sm1[:, 2, :], sm1[:, 2, :], ALU.mult), ("sq", s))
                    chain(dve.scalar_tensor_tensor(sm1[:, 5, :], sm1[:, 4, :], float(D // 4), sm1[:, 1, :],
                                                   ALU.mult, ALU.add), ("var", s))
                    dve.tensor_scalar(sm1[:, 6, :], sm1[:, 5, :], 1.0 / D, EPS, ALU.mult, ALU.add) \
                        .then_inc(*row_step.mark(("eps", s)))
                    dve.wait_ge(*pool_step.past(tok, ("rstd", s)))
                    for i in range(TT):
                        ins = dve.tensor_scalar(dst[:, i, :], src[:, i, :], sm1[:, 3, i:i + 1], sm1[:, 7, i:i + 1],
                                                ALU.subtract, ALU.mult)
                    ins.then_inc(*row_step.mark(("z", s)))

                def split_rows(m, a, step):
                    w = whole[m]
                    if step == "whole":
                        for half in range(2):
                            dve.wait_ge(*sm_filled.past(tok, (m, a, half)))
                            b = sm_bank().rearrange("p (i d) -> p i d", i=2)
                            d = w[:, 2 * half:2 * half + 2]
                            if a == 4:
                                ins = dve.tensor_copy(d, b)
                            else:
                                ins = dve.tensor_tensor(d, b, rows_n(f"b{m}{a}", 2), ALU.add)
                            ins.then_inc(*sm_drained.mark((m, a, half)))
                    if step == "rest":
                        dve.wait_ge(*split.past(tok, ("h", m, a)))
                        dve.wait_ge(*st_filled.past(tok, ("high", m, a)))
                        dve.tensor_tensor(in_heads(w), in_heads(w), part(m, "h")[:, :, 0, :], ALU.subtract) \
                            .then_inc(*row_step.mark(("rest", m, a)))
                    if step == "low":
                        dve.wait_ge(*split.past(tok, ("m", m, a)))
                        dve.tensor_tensor(part(m, "l")[:, :, 0, :], in_heads(w), part(m, "m")[:, :, 0, :], ALU.subtract) \
                            .then_inc(*row_step.mark(("l", m, a)))

                def split_keys(a):
                    for step in ("whole", "rest", "low"):
                        split_rows("k", a, step)

                def maxima(a, h, blocks=range(TT)):
                    kind = ATT_KIND[a]
                    for i in blocks:
                        k0 = max(0, i * P - WIN) if kind == WINDOW else 0
                        k1 = TOK if kind == FULL else (i + 1) * P
                        dve.wait_ge(*sm_filled.past(tok, ("max", a, h, i)))
                        dve.tensor_reduce(parts["q"][:, i, h, MAXROW:MAXROW + 1], sm_bank()[:, 0:k1 - k0], AX_X, ALU.max,
                                          negate=True).then_inc(*sm_drained.mark(("max", a, h, i)))

                def normalise(a, g):
                    dve.wait_ge(*sm_filled.past(tok, ("out", a, g)))
                    b = sm_bank().rearrange("p (i h c) -> p i h c", i=TT, h=GRP)
                    if g:
                        dve.wait_ge(*sm_drained.past(tok, ("out", a, g - 1)))
                    chain(dve.reciprocal(rec[:], b[:, :, :, HD]), ("rec", a, g))
                    w = GRP * HD
                    dve.tensor_tensor(y[:, :, g * w:(g + 1) * w].rearrange("p i (h c) -> p i h c", c=HD),
                                      b[:, :, :, 0:HD], rec[:].unsqueeze(3).to_broadcast([P, TT, GRP, HD]),
                                      ALU.mult).then_inc(*sm_drained.mark(("out", a, g)))

                def attend(a, s):
                    if ATT_KV[a] == "x":
                        split_keys(a)
                    dve.wait_ge(*pool_step.past(tok, ("x", s - 1)))
                    split_rows("q", a, "whole")
                    split_rows("q", a, "rest")
                    maxima(a, 0)
                    split_rows("q", a, "low")
                    maxima(a, 1)
                    for h in range(H):
                        if h + AHEAD < H:
                            maxima(a, h + AHEAD, range(2))
                        if sums_turn(h) is not None:
                            normalise(a, sums_turn(h))
                        if h + AHEAD < H:
                            maxima(a, h + AHEAD, range(2, TT))
                    normalise(a, H // GRP - 1)

                dve.wait_ge(c_in, (tok // 32) + 16)
                norm_rows("ctx", ctok, ctok)
                for s, (kind, n, norm) in enumerate(SUBS):
                    if kind == "att":
                        attend(n, s)
                    dve.wait_ge(*pool_step.past(tok, ("x", s - 1)))
                    if kind == "pre":
                        norm_rows(s, x, y)
                    else:
                        for i in range(TT):
                            dve.wait_ge(*sm_filled.past(tok, ("rows", s, i)))
                            dve.tensor_tensor(y[:, i, :], sm_bank()[:, 0:D], x[:, i, :], ALU.add) \
                                .then_inc(*sm_drained.mark(("rows", s, i)))
                        if norm is not None:
                            dve.wait_ge(*sm_drained.past(tok, ("rows", s, TT - 1)))
                            norm_rows(s, y, y)
                    if early_kv(s):
                        split_keys(SUBS[s + 1][1])
                for sig in (sm_drained, row_step):
                    sig.fill(dve)

        @block.gpsimd
        def _(pool):
            nc.gpsimd.memset(ones[:], 1.0).then_inc(pool_ready, 1)
            nc.gpsimd.memset(m_half[:], -0.5)
            nc.gpsimd.memset(va[:], 0.0)
            nc.gpsimd.memset(parts["q"][:], 0.0)
            nc.gpsimd.memset(parts["k"][:], 0.0)
            pool.drain()
            nc.gpsimd.memset(va[:, :, :, HD:HD + 1], 1.0)
            nc.gpsimd.memset(parts["k"][:, :, :, MAXROW:MAXROW + 1], 1.0).then_inc(pool_ready, 1)
            pool.wait_ge(pool_ready, 2)
            pool.wait_ge(ready, 1)

            pool_step.open(pool)
            with pool.Fori(0, B * TOK, TOK) as tok:
                def rstd(s):
                    pool.wait_ge(*row_step.past(tok, ("eps", s)))
                    pool.tensor_tensor(sm1[:, 7, :], sm1[:, 6, :], m_half[:], ALU.pow) \
                        .then_inc(*pool_step.mark(("rstd", s)))

                rstd("ctx")
                pool.wait_ge(x_in, (tok // 32) + 16)
                pool.tensor_tensor(x, x, rows_n("bo0", TT), ALU.add).then_inc(*pool_step.mark(("x", -1)))
                for s, (kind, n, norm) in enumerate(SUBS):
                    if norm is None:
                        pool.wait_ge(*sm_drained.past(tok, ("rows", s, TT - 1)))
                        pool.tensor_tensor(x, y, rows_n("b2_2" if kind == "att" else "bo5", TT), ALU.add) \
                            .then_inc(*pool_step.mark(("x", s)))
                        continue
                    rstd(s)
                    pool.wait_ge(*row_step.past(tok, ("z", s)))
                    if kind == "pre":
                        pool.tensor_tensor(x, x, rows_n("bo4", TT), ALU.add).then_inc(*pool_step.mark(("x", s)))
                        continue
                    pool.tensor_tensor(x, y, rows_n(f"g{norm}", TT), ALU.mult).then_inc(*pool_step.mark(("g", s)))
                    pool.wait_ge(*pool_step.past(tok, ("g", s)))
                    pool.tensor_tensor(x, x, rows_n(f"b{norm}", TT), ALU.add) \
                        .then_inc(*pool_step.mark("out" if s == len(SUBS) - 1 else ("x", s)))
                pool_step.fill(pool)

    return {name: s.seen for name, s in signals.items()}


def kernel(**inputs):
    import numpy as np
    import ml_dtypes
    import concourse.bacc as bacc
    from concourse.bass_utils import run_bass_kernel_spmd as run

    inp = {k: np.asarray(v) for k, v in inputs.items()}
    L0, L1, L2, L3 = (lambda n, l=l: inp[f"L{l}_xattn_{n}"] for l in range(4))

    def mat(w):
        k = w.shape[0] // P
        return w.reshape(k, P, w.shape[1]).transpose(1, 0, 2).reshape(P, -1)

    def colv(v):
        return v.reshape(-1, P).T

    def heads(w):
        return w.reshape(D, D).T

    zeros = np.zeros(D, np.float32)
    kv2 = L2("Wkv")
    square = {}
    for a, (l, pre) in {0: (L0, "s"), 1: (L0, "c")}.items():
        for m in "qkvo":
            square[f"{m}{a}"] = l(f"{pre}w{m}")
    for a, pre in ((2, "m"), (3, "c")):
        square[f"o{a}"] = L1(f"{pre}_Wo").T
        for m in "qkv":
            square[f"{m}{a}"] = np.zeros((D, D), np.float32)
    square.update(q4=L2("Wq").T, k4=kv2[:D].T, v4=kv2[D:].T, o4=L2("Wo").T)
    for m in "qkvo":
        square[f"{m}5"] = L3(f"W{m}")
    outer = {f"{m}{a}": heads(L1(f"{pre}_W{m}")) for a, pre in ((2, "m"), (3, "c")) for m in "qkv"}
    inner = {f"{m}{a}": L1(f"{pre}_{m}_W") for a, pre in ((2, "sa"), (3, "ca")) for m in "qkv"}

    vec = {}
    for a, l, names in ((0, L0, "sb{}"), (1, L0, "cb{}"), (5, L3, "b{}")):
        for m in "qkvo":
            vec[f"b{m}{a}"] = l(names.format(m))
    for a, pre, ipre in ((2, "m", "sa"), (3, "c", "ca")):
        for m in "qkv":
            vec[f"b{m}{a}"] = L1(f"{pre}_b{m}").reshape(D)
            vec[f"in_{m}{a}"] = L1(f"{ipre}_{m}_b")
        vec[f"bo{a}"] = L1(f"{pre}_bo")
    for m in "qkv":
        vec[f"b{m}4"] = zeros
    vec["bo4"] = L2("bo")
    vec.update(b1_0=L0("b1"), b1_1=L1("ff_b1"), b1_2=L2("b1"), b2_0=L0("b2"), b2_1=L1("ff_b2"), b2_2=L2("b2"))
    norms = [(L0("g1"), L0("be1")), (L0("g2"), L0("be2")), (L0("g3"), L0("be3")),
             (L1("ln1_g"), L1("ln1_b")), (L1("ln2_g"), L1("ln2_b")), (L1("ln3_g"), L1("ln3_b")),
             (L2("ln_q_g"), L2("ln_q_b")), (L3("gamma"), L3("beta")), (L2("ln_kv_g"), L2("ln_kv_b"))]
    for n, (g, b) in enumerate(norms):
        vec[f"g{n}"], vec[f"b{n}"] = g, b

    i, j = np.arange(P)[:, None], np.arange(P)[None, :]
    c, w = np.arange(WCOL)[None, :], np.arange(2 * P)[None, :]
    hide = lambda m: np.where(m, np.float32(-1e30), np.float32(0))
    table = {
        "eye": np.eye(P), "hide_kq": hide(i > j), "hide_qk": hide(j > i),
        "whide_kq": hide((i > w) | (w - i >= WIN)),
        "whide_qk": hide(np.where(c < WIN, c <= i, (c - WIN > i) | (i - (c - WIN) >= WIN))),
        "zeros": np.zeros((P, PAIR)),
        "ones3": np.broadcast_to((i % 32) < 3, (P, P)),
        "next_block": np.where(i % 32 < 3, 1, np.where(i % 32 < 6, w >= P, 0)),
    }

    def parts(v):
        out = []
        v = v.astype(np.float32)
        for _ in range(3):
            h = v.astype(ml_dtypes.bfloat16)
            out.append(h)
            v = v - h.astype(np.float32)
        return out

    slope_k = np.zeros((P, 4, P), ml_dtypes.bfloat16)
    slope_row = np.zeros((P, 4, WCOL), ml_dtypes.bfloat16)
    for h in range(H):
        t, r, p = h // 8, h % 8 // 2, h % 2
        slope = np.float32(2.0 ** (-8.0 * (h + 1) / H)) / np.float32(HD ** -0.5)
        for n in range(3):
            slope_k[32 * r + n, 2 * t + p] = parts(slope * np.arange(P))[n]
            slope_k[32 * r + 3 + n, 2 * t + p] = parts(np.full(P, -P * slope))[n]
            slope_row[32 * r + n, 2 * t + p] = parts(slope * (np.arange(WCOL) - WIN))[n]
    table["slope_k"], table["slope_row"] = slope_k.reshape(P, -1), slope_row.reshape(P, -1)

    def spread(v):
        return np.broadcast_to(v[None, :], (P, v.shape[0]))

    arrays = {
        "x_rows": inp["x"], "x_cols": inp["x"].transpose(0, 2, 1),
        "c_rows": inp["ctx_1024"], "c_cols": inp["ctx_1024"].transpose(0, 2, 1),
        "squares": np.concatenate([mat(square[n]) for n in SQ], 1),
        "folds_a": np.concatenate([mat(inner[n]) for n in FOLDS], 1),
        "folds_b": np.concatenate([mat(outer[n]) for n in FOLDS], 1),
        "w1": np.concatenate([mat(w) for w in (L0("w1"), L1("ff_W1").T, L2("W1").T)], 1),
        "w2": np.concatenate([mat(w) for w in (L0("w2"), L1("ff_W2").T, L2("W2").T)], 1),
        "cols": np.concatenate([colv(vec[n]) for n, _ in COLS], 1),
        "rows": np.concatenate([spread(vec[n]) for n in ROWS], 1),
        "tables": np.concatenate([np.asarray(table[n]).astype(ml_dtypes.bfloat16) for n, _ in TABLES], 1),
        "eye32": np.eye(P, dtype=np.float32),
        "parity": np.stack([(np.arange(P) // HD % 2 == p) for p in range(2)], 1).astype(np.float32),
    }
    arrays = {k: np.ascontiguousarray(v) for k, v in arrays.items()}

    def build(places):
        nc = bacc.Bacc("TRN2", target_bir_lowering=False, num_devices=1)
        args = [nc.dram_tensor(f"{k}_dram", v.shape, mybir.dt.from_np(v.dtype), kind="ExternalInput").ap()
                for k, v in arrays.items()]
        args.append(nc.dram_tensor("out_dram", (B, TOK, D), F32, kind="ExternalOutput").ap())
        return nc, program(nc, places, *args)

    _, places = build({})
    nc, _ = build(places)
    r = run(nc, [{f"{k}_dram": v for k, v in arrays.items()}], core_ids=[0])
    return r.results[0]["out_dram"]
```

```python
from contextlib import ExitStack

import concourse.bass as bass
from concourse import mybir
from concourse.alu_op_type import AluOpType as ALU

F32 = mybir.dt.float32
BF16 = mybir.dt.bfloat16
ACT = mybir.ActivationFunctionType
AX_X = mybir.AxisListType.X

P = 128
B, TOK, D, H, HD, FF = 8, 512, 256, 16, 16, 1024
KT = D // P
TT = TOK // P
FT = FF // P
HALF = TOK // 2
WIN = 64
WCOL = P + WIN
HT = H // KT
PAIR = 2 * HD
GRP = 4
AHEAD = GRP + 1
STEPS = H // GRP * TT
EPS = 1e-5
STEP = TOK

FULL, CAUSAL, WINDOW = range(3)
ATT_KIND = [WINDOW, FULL, CAUSAL, FULL, FULL, FULL]
ATT_SCALE = [HD ** -0.5, HD ** -0.5, D ** -0.5, D ** -0.5, HD ** -0.5, HD ** -0.5]
ATT_KV = ["x", "ctx", "x", "ctx", "nctx", "ctx"]
FFN_ACT = [ACT.Gelu, ACT.Gelu, ACT.Silu]
NEXT_KEYS = {0: 1, 2: 3, 3: 4, 4: 5}
KEY_STEP = H - GRP - 1
LATE_PARTS = 1
SUBS = [("att", 0, 0), ("att", 1, 1), ("ffn", 0, 2), ("att", 2, 3), ("att", 3, 4), ("ffn", 1, 5),
        ("pre", 0, 6), ("att", 4, None), ("ffn", 2, None), ("att", 5, 7)]
TURNS = [s + 1 < len(SUBS) and SUBS[s + 1][0] != "pre" for s in range(len(SUBS))]
KV_NORM = 8


def span(kind, k):
    return k * P if kind != FULL else 0, min(TOK, (k + 2) * P) if kind == WINDOW else TOK


def halves(kind, k):
    q0, q1 = span(kind, k)
    return [range(0, 2), range(2, GRP)] if q1 - q0 > TOK // 2 else [range(GRP)]


def column(kind, k, j):
    q0, q1 = span(kind, k)
    return j * TOK if len(halves(kind, k)) == 2 else j // 2 * TOK + j % 2 * (q1 - q0)


def early_scores(kind):
    return [n for n in range(2) if len(halves(kind, n)) == 2]


def sums_turn(n):
    return n // TT - 1 if n >= TT and n % TT == 2 else None


PART = {"k": {"h": (0, 1, 2), "m": (3, 4), "l": (5,)}, "q": {"h": (1, 3, 5), "m": (2, 4), "l": (0,)}}
MAXROW = 6 * HD
SQ = [f"{m}{a}" for a in range(6) for m in ("q", "k", "v", "o")]
FOLDS = [f"{m}{a}" for a in (2, 3) for m in ("q", "k", "v")]
COLS = ([(f"bv{a}", KT) for a in range(6)]
        + [(f"in_{n}", KT) for n in FOLDS] + [(f"b1_{f}", FT) for f in range(3)]
        + [(f"g{n}", KT) for n in range(9)] + [(f"b{n}", KT) for n in range(9)])
ROWS = ([f"{m}{a}" for m in ("bq", "bk") for a in (0, 1, 2, 3, 5)]
        + [f"bo{a}" for a in range(6)] + [f"b2_{f}" for f in range(3)]
        + [f"{m}{n}" for m in "gb" for n in (0, 1, 2, 3, 4, 5, 7)])
TABLES = [("eye", P), ("hide_kq", P), ("hide_qk", P), ("whide_kq", 2 * P), ("whide_qk", WCOL), ("slope_k", 4 * P),
          ("next_block", 2 * P), ("slope_row", 4 * WCOL), ("ones3", P), ("zeros", PAIR)]


def offsets(names):
    at, out = 0, {}
    for n, w in names:
        out[n] = (at, w)
        at += w
    return out, at


COL_AT, NCOL = offsets(COLS)
ROW_AT, NROW = offsets([(n, D) for n in ROWS])
TAB_AT, NTAB = offsets(TABLES)


class Signal:

    def __init__(self, sem, places):
        self.sem, self.places, self.n, self.seen = sem, places, 1, {}

    def open(self, eng):
        eng.drain().then_inc(self.sem, 1)

    def nth(self, base, n):
        return self.sem, base + (1 + n)

    def mark(self, name, by=1):
        self.n += by
        assert self.n < STEP and name not in self.seen, (name, self.n)
        self.seen[name] = self.n
        return self.sem, by

    def past(self, base, name):
        return self.sem, base + self.places.get(name, 1)

    def fill(self, eng):
        eng.drain().then_inc(self.sem, STEP + 1 - self.n)


def program(nc, places, x_rows, x_cols, c_rows, c_cols, squares, folds_a, folds_b, w1, w2, cols, rows, tables, eye32,
            parity, out):
    nc.disable_value_cache = True
    with ExitStack() as stack:
        def sb(name, shape, dt=F32):
            return stack.enter_context(nc.sbuf_tensor(name, shape, dt))

        def sem(name):
            return stack.enter_context(nc.semaphore(name))

        signals = {}

        def signal(name):
            signals[name] = Signal(sem(name), places.get(name, {}))
            return signals[name]

        sq = sb("sq", [P, len(SQ), KT, D])
        w1s = sb("w1s", [P, KT, FF])
        w2s = sb("w2s", [P, FT, D])
        col = sb("col", [P, NCOL])
        row = sb("row", [P, NROW])
        tab = sb("tab", [P, NTAB], BF16)
        eye = sb("eye", [P, P])
        par = sb("par", [P, 2])
        m_half = sb("m_half", [P, TT])
        ones = sb("ones", [P, P])
        tokens = sb("tokens", [P, 3, TT, D])
        x, y, ctok = tokens[:, 0], tokens[:, 1], tokens[:, 2]
        xT = sb("xT", [P, KT, TOK])
        cT = sb("cT", [P, KT, TOK])
        ncT = sb("ncT", [P, KT, TOK])
        whole = {"k": ctok, "q": y}
        parts = {m: sb(f"{m}_parts", [P, TT, H, P], BF16) for m in "kq"}
        kb = sb("kb", [P, KT, TOK], BF16)
        qb = sb("qb", [P, 2, KT, TOK], BF16)
        turned_parts = sb("turned_parts", [P, 2 * GRP, 2, TOK], BF16)
        va = sb("va", [P, TT, H, PAIR])
        probs = sb("probs", [P, 2, GRP * TOK])
        hid = probs[:].rearrange("p a (r n) -> p (a r) n", n=TOK)
        rec = sb("rec", [P, TT, GRP])
        sums = oT = xT
        st6 = sb("st6", [P, TT, 6])
        sm1 = sb("sm1", [P, 8, TT])

        st = stack.enter_context(nc.psum_tensor("st", [P, 2, 2, TOK], F32))
        pv = stack.enter_context(nc.psum_tensor("pv", [P, TOK], F32))
        tr = stack.enter_context(nc.psum_tensor("tr", [P, 2, TOK], BF16))
        sm = stack.enter_context(nc.psum_tensor("sm", [P, 2, TOK], F32))

        def cv(name):
            a, w = COL_AT[name]
            return col[:, a:a + w]

        def rv(name):
            a, w = ROW_AT[name]
            return row[:, a:a + w]

        def rows_n(name, n):
            return rv(name).unsqueeze(1).to_broadcast([P, n, D])

        def tb(name):
            a, w = TAB_AT[name]
            return tab[:, a:a + w]

        def sqw(name):
            return sq[:, SQ.index(name)]

        def part(m, which):
            g = PART[m][which]
            step = g[1] - g[0] if len(g) > 1 else 1
            rows6 = parts[m][:, :, :, 0:MAXROW].rearrange("p i h (g c) -> p (i h) g c", c=HD)
            return rows6[:, :, g[0]:g[-1] + 1:step, :]

        def group(m, g, at):
            return parts[m][:, :, at, g * HD:(g + 1) * HD]

        def made_late(m, a):
            return m == "q" or ATT_KV[a] == "x"

        def copier(m, a):
            return act_step if m == "q" and ATT_KV[a] == "x" else pool_step

        def in_heads(rows, at=slice(H)):
            return rows.rearrange("p i (h c) -> p i h c", c=HD)[:, :, at, :]

        def split_heads(m, a):
            return [slice(0, HT), slice(HT, H)] if made_late(m, a) else [slice(H)]

        loaded = sem("loaded")
        fold_made = sem("fold_made")
        fold_kept = sem("fold_kept")
        spread = sem("spread")
        ready = sem("ready")
        pool_ready = sem("pool_ready")
        x_in = sem("x_in")
        xT_in = sem("xT_in")
        c_in = sem("c_in")
        cT_in = sem("cT_in")
        w_in = [sem(f"w{f}_in") for f in range(3)]
        stored = sem("stored")
        st_filled = signal("st_filled")
        st_drained = signal("st_drained")
        sm_filled = signal("sm_filled")
        sm_drained = signal("sm_drained")
        tr_filled = signal("tr_filled")
        tr_drained = signal("tr_drained")
        step_done = signal("step_done")
        sums_kept = signal("sums_kept")
        act_step = signal("act_step")
        row_step = signal("row_step")
        pool_step = signal("pool_step")

        N_LOADS = 8
        BIASES = [(f"in_{n}", n, f"b{n}") for n in FOLDS if n[0] != "v"] \
            + [(f"bv{a}", f"o{a}", f"bo{a}") for a in (0, 1, 2, 3, 5)]
        FOLD_JOBS = len(FOLDS) * KT + 2 * KT

        block = stack.enter_context(nc.Block())

        @block.sync
        def _(sp):
            sp.dma_start(tokens[:].rearrange("p a t d -> p (a t d)"), folds_a).then_inc(loaded, 16)
            sp.dma_start(hid.rearrange("p a n -> p (a n)")[:, 0:6 * KT * D], folds_b).then_inc(loaded, 16)
            sp.dma_start(col[:], cols).then_inc(loaded, 16)
            sp.dma_start(row[:], rows).then_inc(loaded, 16)
            sp.dma_start(tab[:], tables).then_inc(loaded, 16)
            sp.dma_start(eye[:], eye32).then_inc(loaded, 16)
            sp.dma_start(par[:], parity).then_inc(loaded, 16)
            sp.dma_start(sq[:].rearrange("p s k n -> p (s k n)"), squares).then_inc(loaded, 16)

        @block.tensor
        def _(pe):
            fa = tokens[:].rearrange("p a t d -> p (a t d)").rearrange("p (j k n) -> p j k n", j=6, k=KT)
            fb = hid.rearrange("p a n -> p (a n)")[:, 0:6 * KT * D].rearrange("p (j k n) -> p j k n", j=6, k=KT)
            pe.wait_ge(loaded, 16 * N_LOADS)
            job = 0

            def fold_bank(pe):
                if job >= 4:
                    pe.wait_ge(fold_kept, job - 3)
                return st[:, job // 2 % 2, job % 2]

            for j, name in enumerate(FOLDS):
                for t in range(KT):
                    b = fold_bank(pe)
                    for k in range(KT):
                        mm = pe.matmul(b[:, 0:D], fa[:, j, k, t * P:(t + 1) * P], fb[:, j, k, :],
                                       start=(k == 0), stop=(k == KT - 1))
                    mm.then_inc(fold_made, 1)
                    job += 1
                for t in range(KT if name[0] == "v" else 0):
                    b = fold_bank(pe)
                    for k in range(KT):
                        mm = pe.matmul(b[:, 0:1], fb[:, j, k, t * P:(t + 1) * P], cv(f"in_{name}")[:, k:k + 1],
                                       start=(k == 0), stop=(k == KT - 1))
                    mm.then_inc(fold_made, 1)
                    job += 1
            assert job == FOLD_JOBS
            for n, (_, w, _) in enumerate(BIASES):
                b = fold_bank(pe)
                pe.wait_ge(spread, 1 + n)
                for k in range(KT):
                    mm = pe.matmul(b[:, 0:D], xT[:, k, n % 2 * P:(n % 2 + 1) * P],
                                   sqw(w)[:, k, :] if w[0] == "o" else fb[:, FOLDS.index(w), k, :],
                                   start=(k == 0), stop=(k == KT - 1))
                mm.then_inc(fold_made, 1)
                job += 1
            pe.wait_ge(ready, 1)
            pe.wait_ge(pool_ready, 2)

            for sig in (st_filled, sm_filled, tr_filled, step_done):
                sig.open(pe)

            with pe.Fori(0, B * TOK, TOK) as tok:
                jobs = {"st": 0, "sm": 0, "tr": 0, "group": 0}

                def st_pair():
                    n = jobs["st"]
                    jobs["st"] += 1
                    pe.wait_ge(*st_drained.nth(tok, max(n - 1, 0)))
                    return st[:, n % 2]

                def sm_bank():
                    n = jobs["sm"]
                    jobs["sm"] += 1
                    pe.wait_ge(*sm_drained.nth(tok, max(n - 1, 0)))
                    return sm[:, n % 2]

                def tr_bank():
                    pe.wait_ge(*tr_drained.nth(tok, jobs["tr"]))
                    jobs["tr"] += 1
                    return tr

                def turn_half(src, pair, half, wait, name):
                    pe.wait_ge(*wait)
                    for i in range(2):
                        for j in range(KT):
                            at = j * HALF + i * P
                            mm = pe.transpose(pair[:, half, at:at + P], src[:, 2 * half + i, j * P:(j + 1) * P], eye[:])
                    mm.then_inc(*st_filled.mark((*name, half)))

                def project(m, a, src, half, b):
                    for i in range(2):
                        n = 2 * half + i
                        for j in range(KT):
                            mm = pe.matmul(b[:, i * D:(i + 1) * D], src[:, j, n * P:(n + 1) * P],
                                           sqw(f"{m}{a}")[:, j, :], start=(j == 0), stop=(j == KT - 1))
                    return mm

                def project_kq(m, a, src, half):
                    project(m, a, src, half, sm_bank()).then_inc(*sm_filled.mark((m, a, half)))

                def project_v(a, src, pair, half):
                    mm = project("v", a, src, half, pair[:, half])
                    if half:
                        mm.then_inc(*st_filled.mark(("v", a)))

                def input_half(s, half):
                    if s == 0:
                        pe.wait_ge(xT_in, (tok // 32) + 16)
                    elif half == 0:
                        pe.wait_ge(*act_step.past(tok, ("turned", s - 1)))
                    else:
                        pe.wait_ge(*st_drained.past(tok, ("turn", s - 1)))

                def source(a):
                    return {"x": xT, "ctx": cT, "nctx": ncT}[ATT_KV[a]]

                def turn_high(m, a):
                    pair = st_pair()
                    for half in range(2):
                        turn_half(whole[m], pair, half, sm_drained.past(tok, (m, a, half)), ("high", m, a))

                def max_unit(a, h, i):
                    kind = ATT_KIND[a]
                    if (h, i) in ((0, 0), (0, TT // 2), (1, 0)):
                        pe.wait_ge(*act_step.past(tok, ("mask", a, h, 1 if h else i // 2)))
                    k0 = max(0, i * P - WIN) if kind == WINDOW else 0
                    k1 = TOK if kind == FULL else (i + 1) * P
                    t, p = h // HT, h % 2
                    g = slice(h % HT // 2 * PAIR, (h % HT // 2 + 1) * PAIR)
                    b = sm_bank()
                    mm = pe.matmul(b[:, 0:k1 - k0], qb[g, p, t, i * P:(i + 1) * P], kb[g, t, k0:k1],
                                   start=True, stop=(kind == FULL))
                    if kind == CAUSAL:
                        mm = pe.matmul(b[:, i * P:k1], tb("eye"), tb("hide_qk"), start=False, stop=True)
                    if kind == WINDOW:
                        w = WCOL - (k1 - k0)
                        pe.matmul(b[:, 0:k1 - k0], tb("eye"), tb("whide_qk")[:, w:WCOL], start=False, stop=False)
                        z = (2 * t + p) * WCOL
                        mm = pe.matmul(b[:, 0:k1 - k0], tb("ones3")[g, :], tb("slope_row")[g, z + w:z + WCOL],
                                       start=False, stop=True)
                    mm.then_inc(*sm_filled.mark(("max", a, h, i)))

                def turn_parts(a, m, q):
                    if m == "q":
                        pe.wait_ge(*sm_drained.past(tok, ("max", a, 2 * q + 1, TT - 1)))
                    if 2 * q in (0, HT):
                        at = 2 * q // HT if made_late(m, a) else 0
                        pe.wait_ge(*row_step.past(tok, ("l", m, a, at)))
                        if made_late(m, a):
                            pe.wait_ge(*copier(m, a).past(tok, ("copies", m, a)))
                    b = tr_bank()
                    for h in range(2):
                        for i in range(TT):
                            mm = pe.transpose(b[:, h, i * P:(i + 1) * P], parts[m][:, i, 2 * q + h, :], tb("eye"))
                    mm.then_inc(*tr_filled.mark(("parts", m, a, q)))

                def scores(a, n, e):
                    kind = ATT_KIND[a]
                    g, k = divmod(n, TT)
                    q0, q1 = span(kind, k)
                    heads = halves(kind, k)[e]
                    pe.wait_ge(*tr_drained.past(tok, ("parts", "q", a, (g * GRP + heads[-1]) // 2)))
                    pair = st_pair().rearrange("p b n -> p (b n)")
                    for j in heads:
                        h = g * GRP + j
                        kk, qq = turned_parts[:, h % (2 * GRP), 0], turned_parts[:, h % (2 * GRP), 1]
                        c = column(kind, k, j) % (2 * TOK)
                        w = q1 - q0
                        mm = pe.matmul(pair[:, c:c + w], kk[:, k * P:(k + 1) * P], qq[:, q0:q1], start=True,
                                       stop=(kind == FULL))
                        if kind == CAUSAL:
                            mm = pe.matmul(pair[:, c:c + P], tb("eye"), tb("hide_kq"), start=False, stop=True)
                        if kind == WINDOW:
                            z = (2 * (h // HT) + h % 2) * P
                            r = h % HT // 2 * PAIR
                            pe.matmul(pair[:, c:c + w], tb("eye"), tb("whide_kq")[:, 0:w], start=False, stop=False)
                            mm = pe.matmul(pair[:, c:c + w], tb("slope_k")[r:r + PAIR, z:z + P],
                                           tb("next_block")[r:r + PAIR, 0:w], start=False, stop=True)
                    mm.then_inc(*st_filled.mark(("scores", a, n, e)))

                def values(a, n):
                    kind = ATT_KIND[a]
                    g, k = divmod(n, TT)
                    q0, q1 = span(kind, k)
                    pe.wait_ge(*st_drained.past(tok, ("probs", a, n, len(halves(kind, k)) - 1)))
                    if k == 0:
                        pe.wait_ge(*sums_kept.nth(tok, jobs["group"]))
                        jobs["group"] += 1
                    if k == 0 and kind == WINDOW:
                        for j in range(GRP):
                            pe.matmul(pv[j * PAIR:(j + 1) * PAIR, :], tb("zeros"), tab[:, 0:TOK], start=True, stop=False)
                    for j in range(GRP):
                        c = column(kind, k, j)
                        mm = pe.matmul(pv[j * PAIR:(j + 1) * PAIR, q0:q1], va[:, k, g * GRP + j, :],
                                       probs[:, n % 2, c:c + q1 - q0],
                                       start=(k == 0 and kind != WINDOW), stop=(k == TT - 1))
                    mm.then_inc(*step_done.mark((a, n)))

                def turn_sums(a, g):
                    pe.wait_ge(*sums_kept.past(tok, (a, g)))
                    b = sm_bank()
                    for i in range(TT):
                        mm = pe.transpose(b[:, i * P:(i + 1) * P], sums[:, g % 2, i * P:(i + 1) * P], eye[:])
                    mm.then_inc(*sm_filled.mark(("out", a, g)))

                def attend(a, s):
                    own = ATT_KV[a] == "x"
                    for half in range(2):
                        input_half(s, half)
                        if own:
                            project_kq("k", a, xT, half)
                        project_kq("q", a, xT, half)
                    if own:
                        turn_high("k", a)
                    turn_high("q", a)

                    def max_units(h, blocks):
                        if h < H:
                            for i in blocks:
                                max_unit(a, h, i)

                    first = early_scores(ATT_KIND[a])
                    if not own:
                        turn_parts(a, "k", 0)
                    max_units(0, range(TT))
                    if own:
                        pair = st_pair()
                        project_v(a, xT, pair, 0)
                    max_units(1, range(TT))
                    if own:
                        max_units(2, range(2))
                        turn_parts(a, "k", 0)
                    else:
                        turn_parts(a, "k", 1)
                        max_units(2, range(2))
                    turn_parts(a, "q", 0)
                    if own:
                        project_v(a, xT, pair, 1)
                    max_units(2, range(2, TT))
                    max_units(3, [0])
                    for n in first[:1]:
                        scores(a, n, 0)
                    max_units(3, [1, 2])
                    if own:
                        turn_parts(a, "k", 1)
                    for n in first[1:]:
                        scores(a, n, 0)
                    max_units(3, [3])
                    max_units(4, range(2))
                    turn_parts(a, "q", 1)
                    max_units(4, range(2, TT))
                    for n in range(STEPS):
                        two = len(halves(ATT_KIND[a], n % TT)) == 2
                        if n not in first:
                            scores(a, n, 0)
                        max_units(n + AHEAD, [0])
                        if two:
                            scores(a, n, 1)
                        max_units(n + AHEAD, [1])
                        if sums_turn(n) is not None:
                            turn_sums(a, sums_turn(n))
                        if n:
                            values(a, n - 1)
                        max_units(n + AHEAD, [2])
                        if n + GRP < H:
                            turn_parts(a, "kq"[n % 2], (n + GRP) // 2)
                        max_units(n + AHEAD, [3])
                        if a in NEXT_KEYS and n == KEY_STEP:
                            if NEXT_KEYS[a] == 1:
                                pe.wait_ge(cT_in, (tok // 32) + 16)
                            if NEXT_KEYS[a] == 4:
                                pe.wait_ge(*st_drained.past(tok, ("turn", "ctx")))
                            for half in range(2):
                                project_kq("k", NEXT_KEYS[a], source(NEXT_KEYS[a]), half)
                        if a in NEXT_KEYS and n == KEY_STEP + 1:
                            turn_high("k", NEXT_KEYS[a])
                    values(a, STEPS - 1)
                    turn_sums(a, H // GRP - 1)
                    pair = st_pair()
                    for t in range(KT):
                        pe.wait_ge(*sm_drained.past(tok, ("out", a, (t + 1) * HT // GRP - 1)))
                        for i in range(TT):
                            mm = pe.transpose(pair[:, t, i * P:(i + 1) * P], y[:, i, t * P:(t + 1) * P], eye[:])
                        mm.then_inc(*st_filled.mark(("oT", a, t)))

                def rows_out(s, src, weight, n, waits):
                    for i in range(TT):
                        if i % 2 == 0:
                            pe.wait_ge(*st_drained.past(tok, waits[i // 2]))
                        b = sm_bank()
                        for j in range(n):
                            mm = pe.matmul(b[:, 0:D], src[:, j, i * P:(i + 1) * P], weight[:, j, :],
                                           start=(j == 0), stop=(j == n - 1))
                        mm.then_inc(*sm_filled.mark(("rows", s, i)))

                def turn_rows(s, src, norm, nxt=None):
                    if nxt:
                        values_pair = st_pair()
                    pair = st_pair()
                    for half in range(2):
                        if nxt:
                            project_v(nxt, source(nxt), values_pair, half)
                        done = ("rows" if norm is None else "z", s, 2 * half + 1)
                        turn_half(src, pair, half, (sm_drained if norm is None else row_step).past(tok, done), ("turn", s))

                for s, (kind, n, norm) in enumerate(SUBS):
                    if kind == "att":
                        attend(n, s)
                        rows_out(s, oT, sqw(f"o{n}"), KT, [("oT", n)] * 2)
                    elif kind == "ffn":
                        pe.wait_ge(w_in[n], (tok // 16) + 32)
                        for half in range(2):
                            input_half(s, half)
                            for c in range(FT // 4):
                                pair = st_pair().rearrange("p b (e n) -> p (b e) n", e=2)
                                for e in range(4):
                                    f = 4 * c + e
                                    for k in range(KT):
                                        mm = pe.matmul(pair[:, e], w1s[:, k, f * P:(f + 1) * P],
                                                       xT[:, k, half * HALF:(half + 1) * HALF],
                                                       start=(k == 0), stop=(k == KT - 1))
                                mm.then_inc(*st_filled.mark(("hid", n, half, c)))
                        if n == 0:
                            turn_rows("ctx", ctok, KV_NORM)
                        rows_out(s, hid, w2s, FT, [("hid", n, half, FT // 4 - 1) for half in range(2)])
                    if TURNS[s]:
                        turn_rows(s, y, norm, NEXT_KEYS.get(n) if kind == "att" else None)
                for sig in (st_filled, sm_filled, tr_filled, step_done):
                    sig.fill(pe)

        @block.scalar
        def _(act):
            act.wait_ge(ready, 1)
            act.wait_ge(pool_ready, 2)
            for sig in (st_drained, tr_drained, act_step, sums_kept):
                sig.open(act)

            def rows_of(array, n):
                return array[bass.ds(n, 1)].rearrange("o (t p) d -> p (o t) d", p=P)

            def cols_of(array, n):
                return array[bass.ds(n, 1)].rearrange("o (k p) n -> p (o k) n", p=P)

            def load_weights(f):
                act.dma_start(w1s[:].rearrange("p k n -> p (k n)"), w1[:, f * KT * FF:(f + 1) * KT * FF]) \
                    .then_inc(w_in[f], 16)
                act.dma_start(w2s[:].rearrange("p k n -> p (k n)"), w2[:, f * FT * D:(f + 1) * FT * D]) \
                    .then_inc(w_in[f], 16)

            act.dma_start(xT[:], cols_of(x_cols, 0)).then_inc(xT_in, 16)
            act.dma_start(cT[:], cols_of(c_cols, 0)).then_inc(cT_in, 16)
            act.dma_start(x, rows_of(x_rows, 0)).then_inc(x_in, 16)
            load_weights(0)
            with act.Fori(0, B) as batch:
                tok = batch * TOK
                jobs = {"st": 0}

                def pair_of():
                    jobs["st"] += 1
                    return st[:, (jobs["st"] - 1) % 2]

                def in_tiles(pair):
                    return pair.rearrange("p h (j n) -> p h j n", j=KT)

                def turned(s, dst, norm, pair, half):
                    act.wait_ge(*st_filled.past(tok, ("turn", s, half)))
                    at = slice(half * HALF, (half + 1) * HALF)
                    for j in range(KT):
                        if norm is None:
                            i = act.activation(dst[:, j, at], in_tiles(pair)[:, half, j], ACT.Identity)
                        else:
                            i = act.activation(dst[:, j, at], in_tiles(pair)[:, half, j], ACT.Identity,
                                               bias=cv(f"b{norm}")[:, j:j + 1], scale=cv(f"g{norm}")[:, j:j + 1])
                    i.then_inc(*(st_drained.mark(("turn", s)) if half else act_step.mark(("turned", s))))

                def split_part(m, a, which, e=0):
                    if which == "h":
                        act.wait_ge(*sm_drained.past(tok, (m, a, 1)))
                    else:
                        act.wait_ge(*row_step.past(tok, ("rest", m, a, e)))
                    if made_late(m, a):
                        at = split_heads(m, a)[e] if which == "m" else slice(H)
                        for g in PART[m][which] if which == "m" else PART[m][which][:1]:
                            i = act.activation(group(m, g, at), in_heads(whole[m], at), ACT.Identity)
                    else:
                        dst = part(m, which)
                        src = whole[m].rearrange("p i (h c) -> p (i h) c", c=HD)
                        i = act.activation(dst, src.unsqueeze(2).to_broadcast(list(dst.shape)), ACT.Identity)
                    i.then_inc(*act_step.mark((which, m, a, e)))

                def values_kept(a, pair):
                    act.wait_ge(*st_filled.past(tok, ("v", a)))
                    act.activation(va[:, :, :, 0:HD].rearrange("p i h c -> p (i h) c"),
                                   pair.rearrange("p b (i h c) -> p (b i h) c", i=2, c=HD), ACT.Identity) \
                        .then_inc(*st_drained.mark(("v", a)))

                def high_keys(a):
                    act.wait_ge(*st_filled.past(tok, ("high", "k", a, 1)))
                    act.activation(kb[:].rearrange("p j (h n) -> p h j n", h=2), in_tiles(pair_of()), ACT.Identity) \
                        .then_inc(*st_drained.mark(("high", "k", a)))

                def attend(a):
                    def parts_kept(m, q):
                        act.wait_ge(*tr_filled.past(tok, ("parts", m, a, q)))
                        slot = 2 * q % (2 * GRP)
                        act.activation(turned_parts[:, slot:slot + 2, "kq".index(m)], tr[:], ACT.Identity) \
                            .then_inc(*tr_drained.mark(("parts", m, a, q)))

                    own = ATT_KV[a] == "x"
                    if own:
                        high_keys(a)
                    pair = pair_of()
                    for half in range(2):
                        act.wait_ge(*st_filled.past(tok, ("high", "q", a, half)))
                        at = slice(half * HALF, (half + 1) * HALF)
                        act.activation(qb[:, 0, :, at], in_tiles(pair)[:, half], ACT.Identity, scale=par[:, 0:1]) \
                            .then_inc(*act_step.mark(("mask", a, 0, half)))
                    act.activation(qb[:, 1].rearrange("p j (h n) -> p h j n", h=2), in_tiles(pair), ACT.Identity,
                                   scale=par[:, 1:2]) \
                        .then_inc(*act_step.mark(("mask", a, 1, 1)))
                    act.drain().then_inc(*st_drained.mark(("high", "q", a)))
                    if own:
                        split_part("k", a, "h")
                    split_part("q", a, "h")
                    if own:
                        split_part("k", a, "m")
                    else:
                        parts_kept("k", 0)
                    split_part("q", a, "m")
                    if own:
                        dst = part("q", "h")[:, :, 1:, :]
                        act.activation(dst, part("q", "h")[:, :, 0:1, :].to_broadcast(list(dst.shape)), ACT.Identity) \
                            .then_inc(*act_step.mark(("copies", "q", a)))
                    else:
                        parts_kept("k", 1)

                    def keep_sums(g):
                        act.wait_ge(*step_done.past(tok, (a, (g + 1) * TT - 1)))
                        if g >= 2:
                            act.wait_ge(*sm_filled.past(tok, ("out", a, g - 2)))
                        act.activation(sums[:, g % 2, :], pv[:], ACT.Identity).then_inc(*sums_kept.mark((a, g)))

                    def exponentials(n, e):
                        kind = ATT_KIND[a]
                        k = n % TT
                        heads = halves(kind, k)[e]
                        q0, q1 = span(kind, k)
                        w = (q1 - q0) * len(heads) // 2
                        if n >= 2:
                            act.wait_ge(*step_done.past(tok, (a, n - 2)))
                        act.wait_ge(*st_filled.past(tok, ("scores", a, n, e)))
                        c = column(kind, k, heads[0])
                        dst = probs[:, n % 2, c:c + 2 * TOK].rearrange("p (b n) -> p b n", b=2)
                        act.activation(dst[:, :, 0:w], pair_of()[:, :, 0:w], ACT.Exp, scale=ATT_SCALE[a]) \
                            .then_inc(*st_drained.mark(("probs", a, n, e)))

                    first = early_scores(ATT_KIND[a])
                    if own:
                        parts_kept("k", 0)
                    parts_kept("q", 0)
                    if own:
                        values_kept(a, pair_of())
                    for n in first[:1]:
                        exponentials(n, 0)
                    if own:
                        parts_kept("k", 1)
                    for n in first[1:]:
                        exponentials(n, 0)
                    parts_kept("q", 1)
                    for n in range(STEPS):
                        if n not in first:
                            exponentials(n, 0)
                        if n == LATE_PARTS:
                            for m in "kq":
                                if made_late(m, a):
                                    split_part(m, a, "m", 1)
                        if len(halves(ATT_KIND[a], n % TT)) == 2:
                            exponentials(n, 1)
                        if n + GRP < H:
                            parts_kept("kq"[n % 2], (n + GRP) // 2)
                        if n and n % TT == 0:
                            keep_sums(n // TT - 1)
                        if a in NEXT_KEYS and n == KEY_STEP + 1:
                            high_keys(NEXT_KEYS[a])
                    keep_sums(H // GRP - 1)
                    pair = pair_of()
                    for t in range(KT):
                        act.wait_ge(*st_filled.past(tok, ("oT", a, t)))
                        i = act.activation(oT[:, t], pair[:, t], ACT.Identity)
                    i.then_inc(*st_drained.mark(("oT", a)))

                for s, (kind, n, norm) in enumerate(SUBS):
                    if kind == "att":
                        attend(n)
                    elif kind == "ffn":
                        for half in range(2):
                            at = slice(half * HALF, (half + 1) * HALF)
                            for c in range(FT // 4):
                                act.wait_ge(*st_filled.past(tok, ("hid", n, half, c)))
                                pair = pair_of().rearrange("p b (e n) -> p (b e) n", e=2)
                                for e in range(4):
                                    f = 4 * c + e
                                    i = act.activation(hid[:, f, at], pair[:, e], FFN_ACT[n],
                                                       bias=cv(f"b1_{n}")[:, f:f + 1])
                                i.then_inc(*st_drained.mark(("hid", n, half, c)))
                        if n == 0:
                            pair = pair_of()
                            for half in range(2):
                                turned("ctx", ncT, KV_NORM, pair, half)
                        act.wait_ge(*sm_filled.past(tok, ("rows", s, TT - 1)))
                        load_weights((n + 1) % 3)
                    if TURNS[s]:
                        nxt = NEXT_KEYS.get(n) if kind == "att" else None
                        if nxt:
                            split_part("k", nxt, "h")
                            values_pair = pair_of()
                        pair = pair_of()
                        turned(s, xT, norm, pair, 0)
                        if nxt:
                            values_kept(nxt, values_pair)
                        turned(s, xT, norm, pair, 1)
                        if nxt:
                            split_part("k", nxt, "m")
                    if s == 0:
                        act.wait_ge(*row_step.past(tok, ("l", "k", 1, 0)))
                        act.dma_start(ctok, rows_of(c_rows, batch)).then_inc(c_in, 16)
                act.wait_ge(*sm_filled.past(tok, ("rows", len(SUBS) - 1, TT - 1)))
                act.dma_start(xT[:], cols_of(x_cols, batch + 1)).then_inc(xT_in, 16)
                act.dma_start(cT[:], cols_of(c_cols, batch + 1)).then_inc(cT_in, 16)
                act.wait_ge(*pool_step.past(tok, ("x", len(SUBS) - 1, 1)))
                act.dma_start(rows_of(out, batch), x).then_inc(stored, 16)
                act.wait_ge(stored, batch * 16 + 16)
                act.dma_start(x, rows_of(x_rows, batch + 1)).then_inc(x_in, 16)
                for sig in (st_drained, tr_drained, act_step, sums_kept):
                    sig.fill(act)
            for came in (xT_in, cT_in, x_in):
                act.wait_ge(came, 16 * (B + 1))
            act.wait_ge(w_in[0], 32 * (B + 1))

        @block.vector
        def _(dve):
            dve.wait_ge(loaded, 16 * N_LOADS)
            dve.wait_ge(pool_ready, 1)
            job = 0

            def fold_bank():
                dve.wait_ge(fold_made, job + 1)
                return st[:, job // 2 % 2, job % 2]

            for name in FOLDS:
                for t in range(KT):
                    dve.tensor_copy(sqw(name)[:, t, :], fold_bank()[:, 0:D]).then_inc(fold_kept, 1)
                    job += 1
                for t in range(KT if name[0] == "v" else 0):
                    b = cv(f"b{name}")[:, t:t + 1]
                    dve.tensor_tensor(b, fold_bank()[:, 0:1], b, ALU.add).then_inc(fold_kept, 1)
                    job += 1
            dve.wait_ge(fold_kept, job)
            for n, (c, _, to) in enumerate(BIASES):
                for k in range(KT):
                    ins = dve.tensor_scalar(xT[:, k, n % 2 * P:(n % 2 + 1) * P], ones[:], cv(c)[:, k:k + 1], None, ALU.mult)
                ins.then_inc(spread, 1)
                dve.tensor_tensor(rv(to), fold_bank()[:, 0:D], rv(to), ALU.add).then_inc(fold_kept, 1)
                job += 1
            dve.wait_ge(fold_kept, job)
            for b, extra in [("b0", "bo1"), ("b1", "b2_0"), ("b2", "bo2"), ("b3", "bo3"), ("b4", "b2_1")]:
                dve.tensor_tensor(rv(b), rv(b), rv(extra), ALU.add)
            dve.drain().then_inc(ready, 1)

            for sig in (sm_drained, row_step):
                sig.open(dve)
            with dve.Fori(0, B * TOK, TOK) as tok:
                jobs = {"sm": 0}

                def sm_bank():
                    jobs["sm"] += 1
                    return sm[:, (jobs["sm"] - 1) % 2]

                def chain(ins, name):
                    ins.then_inc(*row_step.mark(name))
                    dve.wait_ge(*row_step.past(tok, name))

                def statistics(s, src, half):
                    at = slice(2 * half, 2 * half + 2)
                    for i in (2 * half, 2 * half + 1):
                        ins = dve.bn_stats(st6[:, i, :], src[:, i, :])
                    chain(ins, ("stats", s, half))
                    e, o, me, mo = st6[:, at, 1], st6[:, at, 4], st6[:, at, 2], st6[:, at, 5]
                    dve.tensor_tensor(sm1[:, 0, at], e, o, ALU.add)
                    dve.tensor_tensor(sm1[:, 1, at], me, mo, ALU.add)
                    chain(dve.tensor_tensor(sm1[:, 2, at], e, o, ALU.subtract), ("halves", s, half))
                    dve.tensor_scalar(sm1[:, 3, at], sm1[:, 0, at], 0.5, None, ALU.mult)
                    chain(dve.tensor_tensor(sm1[:, 4, at], sm1[:, 2, at], sm1[:, 2, at], ALU.mult), ("sq", s, half))
                    chain(dve.scalar_tensor_tensor(sm1[:, 5, at], sm1[:, 4, at], float(D // 4), sm1[:, 1, at],
                                                   ALU.mult, ALU.add), ("var", s, half))
                    dve.tensor_scalar(sm1[:, 6, at], sm1[:, 5, at], 1.0 / D, EPS, ALU.mult, ALU.add) \
                        .then_inc(*row_step.mark(("eps", s, half)))

                def normal(s, src, dst, half):
                    dve.wait_ge(*pool_step.past(tok, ("rstd", s, half)))
                    for i in (2 * half, 2 * half + 1):
                        ins = dve.tensor_scalar(dst[:, i, :], src[:, i, :], sm1[:, 3, i:i + 1], sm1[:, 7, i:i + 1],
                                                ALU.subtract, ALU.mult)
                    ins.then_inc(*row_step.mark(("z", s, 2 * half + 1)))

                def whole_rows(m, a, half):
                    dve.wait_ge(*sm_filled.past(tok, (m, a, half)))
                    b = sm_bank().rearrange("p (i d) -> p i d", i=2)
                    d = whole[m][:, 2 * half:2 * half + 2]
                    if a == 4:
                        ins = dve.tensor_copy(d, b)
                    else:
                        ins = dve.tensor_tensor(d, b, rows_n(f"b{m}{a}", 2), ALU.add)
                    ins.then_inc(*sm_drained.mark((m, a, half)))

                def split_rows(m, a, step, e=0):
                    at = split_heads(m, a)[e]
                    w = in_heads(whole[m], at)
                    if step == "rest":
                        dve.wait_ge(*act_step.past(tok, ("h", m, a, 0)))
                        dve.wait_ge(*st_filled.past(tok, ("high", m, a, 1)))
                        dve.tensor_tensor(w, w, group(m, PART[m]["h"][0], at), ALU.subtract) \
                            .then_inc(*row_step.mark(("rest", m, a, e)))
                    if step == "low":
                        dve.wait_ge(*act_step.past(tok, ("m", m, a, e)))
                        dve.tensor_tensor(group(m, PART[m]["l"][0], at), w, group(m, PART[m]["m"][0], at),
                                          ALU.subtract).then_inc(*row_step.mark(("l", m, a, e)))

                def maxima(a, h, blocks=range(TT)):
                    kind = ATT_KIND[a]
                    for i in blocks:
                        k0 = max(0, i * P - WIN) if kind == WINDOW else 0
                        k1 = TOK if kind == FULL else (i + 1) * P
                        dve.wait_ge(*sm_filled.past(tok, ("max", a, h, i)))
                        dve.tensor_reduce(parts["q"][:, i, h, MAXROW:MAXROW + 1], sm_bank()[:, 0:k1 - k0], AX_X, ALU.max,
                                          negate=True).then_inc(*sm_drained.mark(("max", a, h, i)))

                def normalise(a, g):
                    dve.wait_ge(*sm_filled.past(tok, ("out", a, g)))
                    b = sm_bank().rearrange("p (i h c) -> p i h c", i=TT, h=GRP)
                    if g:
                        dve.wait_ge(*sm_drained.past(tok, ("out", a, g - 1)))
                    chain(dve.reciprocal(rec[:], b[:, :, :, HD]), ("rec", a, g))
                    w = GRP * HD
                    dve.tensor_tensor(y[:, :, g * w:(g + 1) * w].rearrange("p i (h c) -> p i h c", c=HD),
                                      b[:, :, :, 0:HD], rec[:].unsqueeze(3).to_broadcast([P, TT, GRP, HD]),
                                      ALU.mult).then_inc(*sm_drained.mark(("out", a, g)))

                def attend(a, s):
                    own = ATT_KV[a] == "x"
                    for half in range(2):
                        if own:
                            whole_rows("k", a, half)
                        dve.wait_ge(*(pool_step.past(tok, ("x", s - 1, half)) if s else pool_step.nth(tok, 0)))
                        whole_rows("q", a, half)
                    if not own:
                        split_rows("k", a, "low")
                    maxima(a, 0)
                    if own:
                        split_rows("k", a, "rest")
                    split_rows("q", a, "rest")
                    maxima(a, 1)
                    if own:
                        split_rows("k", a, "low")
                    split_rows("q", a, "low")
                    for h in range(2, AHEAD):
                        maxima(a, h)
                    for m in "kq":
                        if made_late(m, a):
                            split_rows(m, a, "rest", 1)
                    for n in range(STEPS):
                        if n + AHEAD < H:
                            maxima(a, n + AHEAD, range(2))
                        if sums_turn(n) is not None:
                            normalise(a, sums_turn(n))
                        if n + AHEAD < H:
                            maxima(a, n + AHEAD, range(2, TT))
                        if n == LATE_PARTS:
                            for m in "kq":
                                if made_late(m, a):
                                    split_rows(m, a, "low", 1)
                        if a in NEXT_KEYS and n == KEY_STEP:
                            for half in range(2):
                                whole_rows("k", NEXT_KEYS[a], half)
                    normalise(a, H // GRP - 1)

                for s, (kind, n, norm) in enumerate(SUBS):
                    if kind == "att":
                        attend(n, s)
                    if kind == "ffn" and n == 0:
                        dve.wait_ge(c_in, (tok // 32) + 16)
                        for half in range(2):
                            statistics("ctx", ctok, half)
                        for half in range(2):
                            normal("ctx", ctok, ctok, half)

                    def add_rows(i):
                        dve.wait_ge(*pool_step.past(tok, ("x", s - 1, i // 2)))
                        dve.wait_ge(*sm_filled.past(tok, ("rows", s, i)))
                        dve.tensor_tensor(y[:, i, :], sm_bank()[:, 0:D], x[:, i, :], ALU.add) \
                            .then_inc(*sm_drained.mark(("rows", s, i)))

                    if kind == "pre":
                        for half in range(2):
                            dve.wait_ge(*pool_step.past(tok, ("x", s - 1, half)))
                            statistics(s, x, half)
                        for half in range(2):
                            normal(s, x, y, half)
                    elif norm is None:
                        for i in range(TT):
                            add_rows(i)
                    else:
                        add_rows(0)
                        add_rows(1)
                        dve.wait_ge(*sm_drained.past(tok, ("rows", s, 1)))
                        statistics(s, y, 0)
                        add_rows(2)
                        normal(s, y, y, 0)
                        add_rows(3)
                        dve.wait_ge(*sm_drained.past(tok, ("rows", s, 3)))
                        statistics(s, y, 1)
                        normal(s, y, y, 1)
                    if kind == "att" and n in NEXT_KEYS:
                        split_rows("k", NEXT_KEYS[n], "rest")
                for sig in (sm_drained, row_step):
                    sig.fill(dve)

        @block.gpsimd
        def _(pool):
            nc.gpsimd.memset(ones[:], 1.0).then_inc(pool_ready, 1)
            nc.gpsimd.memset(m_half[:], -0.5)
            nc.gpsimd.memset(va[:], 0.0)
            nc.gpsimd.memset(parts["q"][:], 0.0)
            nc.gpsimd.memset(parts["k"][:], 0.0)
            pool.drain()
            nc.gpsimd.memset(va[:, :, :, HD:HD + 1], 1.0)
            nc.gpsimd.memset(parts["k"][:, :, :, MAXROW:MAXROW + 1], 1.0).then_inc(pool_ready, 1)
            pool.wait_ge(pool_ready, 2)
            pool.wait_ge(ready, 1)

            pool_step.open(pool)
            with pool.Fori(0, B * TOK, TOK) as tok:
                def rstd(s, half):
                    at = slice(2 * half, 2 * half + 2)
                    pool.wait_ge(*row_step.past(tok, ("eps", s, half)))
                    pool.tensor_tensor(sm1[:, 7, at], sm1[:, 6, at], m_half[:, at], ALU.pow) \
                        .then_inc(*pool_step.mark(("rstd", s, half)))

                def copies(m, a):
                    pool.wait_ge(*act_step.past(tok, ("h", m, a, 0)))
                    dst = part(m, "h")[:, :, 1:, :]
                    src = part(m, "h")[:, :, 0:1, :].to_broadcast(list(dst.shape))
                    one = ones[:, 0:1].unsqueeze(2).unsqueeze(3).to_broadcast(list(dst.shape))
                    pool.tensor_tensor(dst, src, one, ALU.mult) \
                        .then_inc(*pool_step.mark(("copies", m, a)))

                pool.wait_ge(x_in, (tok // 32) + 16)
                for half in range(2):
                    pool.tensor_tensor(x[:, 2 * half:2 * half + 2], x[:, 2 * half:2 * half + 2], rows_n("bo0", 2), ALU.add) \
                        .then_inc(*pool_step.mark(("x", -1, half)))
                for s, (kind, n, norm) in enumerate(SUBS):
                    if kind == "att":
                        for m in "kq":
                            if made_late(m, n) and copier(m, n) is pool_step:
                                copies(m, n)
                    if kind == "ffn" and n == 0:
                        for half in range(2):
                            rstd("ctx", half)
                    if kind == "pre":
                        for half in range(2):
                            rstd(s, half)
                    for half in range(2):
                        xs, ys = x[:, 2 * half:2 * half + 2], y[:, 2 * half:2 * half + 2]
                        if norm is None:
                            pool.wait_ge(*sm_drained.past(tok, ("rows", s, 2 * half + 1)))
                            pool.tensor_tensor(xs, ys, rows_n("b2_2" if kind == "att" else "bo5", 2), ALU.add) \
                                .then_inc(*pool_step.mark(("x", s, half)))
                            continue
                        if kind != "pre" and half == 0:
                            rstd(s, 0)
                        pool.wait_ge(*row_step.past(tok, ("z", s, 2 * half + 1)))
                        if kind == "pre":
                            pool.tensor_tensor(xs, xs, rows_n("bo4", 2), ALU.add).then_inc(*pool_step.mark(("x", s, half)))
                            continue
                        pool.tensor_tensor(xs, ys, rows_n(f"g{norm}", 2), ALU.mult).then_inc(*pool_step.mark(("g", s, half)))
                        if half == 0:
                            rstd(s, 1)
                        pool.wait_ge(*pool_step.past(tok, ("g", s, half)))
                        pool.tensor_tensor(xs, xs, rows_n(f"b{norm}", 2), ALU.add) \
                            .then_inc(*pool_step.mark(("x", s, half)))
                pool_step.fill(pool)

    return {name: s.seen for name, s in signals.items()}


def kernel(**inputs):
    import numpy as np
    import ml_dtypes
    import concourse.bacc as bacc
    from concourse.bass_utils import run_bass_kernel_spmd as run

    inp = {k: np.asarray(v) for k, v in inputs.items()}
    L0, L1, L2, L3 = (lambda n, l=l: inp[f"L{l}_xattn_{n}"] for l in range(4))

    def mat(w):
        k = w.shape[0] // P
        return w.reshape(k, P, w.shape[1]).transpose(1, 0, 2).reshape(P, -1)

    def colv(v):
        return v.reshape(-1, P).T

    def heads(w):
        return w.reshape(D, D).T

    zeros = np.zeros(D, np.float32)
    kv2 = L2("Wkv")
    square = {}
    for a, (l, pre) in {0: (L0, "s"), 1: (L0, "c")}.items():
        for m in "qkvo":
            square[f"{m}{a}"] = l(f"{pre}w{m}")
    for a, pre in ((2, "m"), (3, "c")):
        square[f"o{a}"] = L1(f"{pre}_Wo").T
        for m in "qkv":
            square[f"{m}{a}"] = np.zeros((D, D), np.float32)
    square.update(q4=L2("Wq").T, k4=kv2[:D].T, v4=kv2[D:].T, o4=L2("Wo").T)
    for m in "qkvo":
        square[f"{m}5"] = L3(f"W{m}")
    outer = {f"{m}{a}": heads(L1(f"{pre}_W{m}")) for a, pre in ((2, "m"), (3, "c")) for m in "qkv"}
    inner = {f"{m}{a}": L1(f"{pre}_{m}_W") for a, pre in ((2, "sa"), (3, "ca")) for m in "qkv"}

    vec = {}
    for a, l, names in ((0, L0, "sb{}"), (1, L0, "cb{}"), (5, L3, "b{}")):
        for m in "qkvo":
            vec[f"b{m}{a}"] = l(names.format(m))
    for a, pre, ipre in ((2, "m", "sa"), (3, "c", "ca")):
        for m in "qkv":
            vec[f"b{m}{a}"] = L1(f"{pre}_b{m}").reshape(D)
            vec[f"in_{m}{a}"] = L1(f"{ipre}_{m}_b")
        vec[f"bo{a}"] = L1(f"{pre}_bo")
    for m in "qkv":
        vec[f"b{m}4"] = zeros
    vec["bo4"] = L2("bo")
    vec.update(b1_0=L0("b1"), b1_1=L1("ff_b1"), b1_2=L2("b1"), b2_0=L0("b2"), b2_1=L1("ff_b2"), b2_2=L2("b2"))
    norms = [(L0("g1"), L0("be1")), (L0("g2"), L0("be2")), (L0("g3"), L0("be3")),
             (L1("ln1_g"), L1("ln1_b")), (L1("ln2_g"), L1("ln2_b")), (L1("ln3_g"), L1("ln3_b")),
             (L2("ln_q_g"), L2("ln_q_b")), (L3("gamma"), L3("beta")), (L2("ln_kv_g"), L2("ln_kv_b"))]
    for n, (g, b) in enumerate(norms):
        vec[f"g{n}"], vec[f"b{n}"] = g, b

    i, j = np.arange(P)[:, None], np.arange(P)[None, :]
    c, w = np.arange(WCOL)[None, :], np.arange(2 * P)[None, :]
    hide = lambda m: np.where(m, np.float32(-1e30), np.float32(0))
    table = {
        "eye": np.eye(P), "hide_kq": hide(i > j), "hide_qk": hide(j > i),
        "whide_kq": hide((i > w) | (w - i >= WIN)),
        "whide_qk": hide(np.where(c < WIN, c <= i, (c - WIN > i) | (i - (c - WIN) >= WIN))),
        "zeros": np.zeros((P, PAIR)),
        "ones3": np.broadcast_to((i % 32) < 3, (P, P)),
        "next_block": np.where(i % 32 < 3, 1, np.where(i % 32 < 6, w >= P, 0)),
    }

    def parts(v):
        out = []
        v = v.astype(np.float32)
        for _ in range(3):
            h = v.astype(ml_dtypes.bfloat16)
            out.append(h)
            v = v - h.astype(np.float32)
        return out

    slope_k = np.zeros((P, 4, P), ml_dtypes.bfloat16)
    slope_row = np.zeros((P, 4, WCOL), ml_dtypes.bfloat16)
    for h in range(H):
        t, r, p = h // 8, h % 8 // 2, h % 2
        slope = np.float32(2.0 ** (-8.0 * (h + 1) / H)) / np.float32(HD ** -0.5)
        for n in range(3):
            slope_k[32 * r + n, 2 * t + p] = parts(slope * np.arange(P))[n]
            slope_k[32 * r + 3 + n, 2 * t + p] = parts(np.full(P, -P * slope))[n]
            slope_row[32 * r + n, 2 * t + p] = parts(slope * (np.arange(WCOL) - WIN))[n]
    table["slope_k"], table["slope_row"] = slope_k.reshape(P, -1), slope_row.reshape(P, -1)

    def spread(v):
        return np.broadcast_to(v[None, :], (P, v.shape[0]))

    def one_more(v):
        return np.concatenate([v, np.zeros((1, *v.shape[1:]), v.dtype)])

    arrays = {
        "x_rows": one_more(inp["x"]), "x_cols": one_more(inp["x"].transpose(0, 2, 1)),
        "c_rows": inp["ctx_1024"], "c_cols": one_more(inp["ctx_1024"].transpose(0, 2, 1)),
        "squares": np.concatenate([mat(square[n]) for n in SQ], 1),
        "folds_a": np.concatenate([mat(inner[n]) for n in FOLDS], 1),
        "folds_b": np.concatenate([mat(outer[n]) for n in FOLDS], 1),
        "w1": np.concatenate([mat(w) for w in (L0("w1"), L1("ff_W1").T, L2("W1").T)], 1),
        "w2": np.concatenate([mat(w) for w in (L0("w2"), L1("ff_W2").T, L2("W2").T)], 1),
        "cols": np.concatenate([colv(vec[n]) for n, _ in COLS], 1),
        "rows": np.concatenate([spread(vec[n]) for n in ROWS], 1),
        "tables": np.concatenate([np.asarray(table[n]).astype(ml_dtypes.bfloat16) for n, _ in TABLES], 1),
        "eye32": np.eye(P, dtype=np.float32),
        "parity": np.stack([(np.arange(P) // HD % 2 == p) for p in range(2)], 1).astype(np.float32),
    }
    arrays = {k: np.ascontiguousarray(v) for k, v in arrays.items()}

    def build(places):
        nc = bacc.Bacc("TRN2", target_bir_lowering=False, num_devices=1)
        args = [nc.dram_tensor(f"{k}_dram", v.shape, mybir.dt.from_np(v.dtype), kind="ExternalInput").ap()
                for k, v in arrays.items()]
        args.append(nc.dram_tensor("out_dram", (B, TOK, D), F32, kind="ExternalOutput").ap())
        return nc, program(nc, places, *args)

    _, places = build({})
    nc, _ = build(places)
    r = run(nc, [{f"{k}_dram": v for k, v in arrays.items()}], core_ids=[0])
    return r.results[0]["out_dram"]
```
